# Optimizing a Trainium2 kernel written in Bass

```python
import numpy as np
import jax
import jax.numpy as jnp

def _softmax(x, axis=-1):
    return jax.nn.softmax(x, axis=axis)

def _gelu(x):
    return jax.nn.gelu(x, approximate=True)

def _silu(x):
    return jax.nn.silu(x)

def _sigmoid(x):
    return jax.nn.sigmoid(x)

def _layernorm(x, axis=-1, eps=1e-05):
    m = jnp.mean(x, axis=axis, keepdims=True)
    v = jnp.var(x, axis=axis, keepdims=True)
    return (x - m) / jnp.sqrt(v + eps)

def _scatter_add(tgt, idx, src, axis=0):
    return tgt.at[idx].add(src)

def _segment_sum(src, seg, n):
    return jax.ops.segment_sum(src, seg, n)
kernel_name = 'mk_xattn_seq_d4_seqx_r2_bda3bf'

def setup_inputs(seed: int=0):
    np.random.seed(seed)
    _w = jnp.asarray

    def _rec_inputs():
        import jax
        import jax.numpy as jnp
        _rk = jax.random.key(seed)
        x = -0.000125 + 0.9999 * jax.random.normal(jax.random.fold_in(_rk, 1), (8, 512, 512), jnp.float32)
        _lenS = 512 - jax.random.randint(jax.random.fold_in(_rk, 7), (8,), 0, max(1, 512 // 4) + 1, jnp.int32)
        _lenS2 = 77 - jax.random.randint(jax.random.fold_in(_rk, 8), (8,), 0, max(1, 77 // 4) + 1, jnp.int32)
        _ctx_2048P = jax.random.normal(jax.random.fold_in(_rk, 11), (8, 16, 1024), jnp.float32)
        _ctx_2048c = jax.random.dirichlet(jax.random.fold_in(_rk, 511), 0.3 * jnp.ones((16,), jnp.float32), (8, 77))
        _ctx_2048t = jnp.einsum('bsk,bkd->bsd', _ctx_2048c, _ctx_2048P)
        _ctx_2048t = _ctx_2048t * jax.lax.rsqrt(jnp.mean(jnp.square(_ctx_2048t)) + 1e-12) * 0.953939
        ctx_2048 = 5.36139e-06 + 1.00015 * (_ctx_2048t + 0.3 * jax.random.normal(jax.random.fold_in(_rk, 611), (8, 77, 1024), jnp.float32))
        _validS = jnp.arange(512)[None, :] < _lenS[:, None]
        _validS2 = jnp.arange(77)[None, :] < _lenS2[:, None]
        _causal = jnp.tril(jnp.ones((512, 512), dtype=bool))
        mask_S_fk1 = jnp.where(_validS[0], 1.0, 0.0).astype(jnp.float32)
        mask_S_fk0 = jnp.where(_validS[0], 0.0, 1.0).astype(jnp.float32)
        return (x, ctx_2048, mask_S_fk1, mask_S_fk0)
    x, ctx_2048, mask_S_fk1, mask_S_fk0 = _rec_inputs()

    def _L0_xattn_setup():
        import jax, jax.numpy as jnp
        import numpy as np
        HEADS = 16
        HEAD_DIM = 64
        SUPPRESS = 20.0
        key = jax.random.key(seed)
        ks = jax.random.split(key, 8)
        B, HW, C, T, CT = (8, 2048, 512, 77, 1024)
        inner = HEADS * HEAD_DIM
        scale = 0.02
        return {'hidden_states': jax.random.normal(ks[0], (B, HW, C), jnp.float32), 'encoder_hidden_states': jax.random.normal(ks[1], (B, T, CT), jnp.float32), 'mask_A': (jax.random.uniform(ks[2], (HW,)) > 0.5).astype(jnp.float32), 'mask_B': (jax.random.uniform(ks[3], (HW,)) > 0.5).astype(jnp.float32), 'Wq': jax.random.normal(ks[4], (C, inner), jnp.float32) * scale, 'Wk': jax.random.normal(ks[5], (CT, inner), jnp.float32) * scale, 'Wv': jax.random.normal(ks[6], (CT, inner), jnp.float32) * scale, 'Wo': jax.random.normal(ks[7], (inner, C), jnp.float32) * scale, 'bo': jnp.zeros((C,), jnp.float32), 'token_indices_A': jnp.array([2, 3], dtype=jnp.int64), 'token_indices_B': jnp.array([5, 6], dtype=jnp.int64)}
    _L0_xattn_all = _L0_xattn_setup()
    _L0_xattn_in = {k: v for k, v in _L0_xattn_all.items() if k in ('Wq', 'Wk', 'Wv', 'Wo', 'bo', 'token_indices_A', 'token_indices_B')}
    del _L0_xattn_all

    def _L1_xattn_setup():
        import jax, jax.numpy as jnp
        import numpy as np
        D_MODEL = 512
        N_HEADS = 16
        N_KV_HEADS = 4
        HEAD_DIM = D_MODEL // N_HEADS
        SPEAKER_DIM = 1024
        EPS = 1e-05

        def rmsnorm(x, w, eps=EPS):
            xf = x.astype(jnp.float32)
            inv = jax.lax.rsqrt(jnp.mean(xf * xf, axis=-1, keepdims=True) + eps)
            return (xf * inv).astype(x.dtype) * w
        key = jax.random.key(seed)
        ks = jax.random.split(key, 7)
        B, T, S = (4, 1024, 256)
        x = jax.random.normal(ks[0], (B, T, D_MODEL), dtype=jnp.float32)
        cond = jax.random.normal(ks[1], (B, S, SPEAKER_DIM), dtype=jnp.float32)
        sq = 0.02
        wq = jax.random.normal(ks[2], (D_MODEL, N_HEADS * HEAD_DIM), dtype=jnp.float32) * sq
        wk = jax.random.normal(ks[3], (SPEAKER_DIM, N_KV_HEADS * HEAD_DIM), dtype=jnp.float32) * sq
        wv = jax.random.normal(ks[4], (SPEAKER_DIM, N_KV_HEADS * HEAD_DIM), dtype=jnp.float32) * sq
        wo = jax.random.normal(ks[5], (N_HEADS * HEAD_DIM, D_MODEL), dtype=jnp.float32) * sq
        norm_w = jnp.ones((D_MODEL,), dtype=jnp.float32)
        return {'x': x, 'cond': cond, 'wq': wq, 'wk': wk, 'wv': wv, 'wo': wo, 'norm_w': norm_w}
    _L1_xattn_all = _L1_xattn_setup()
    _L1_xattn_in = {k: v for k, v in _L1_xattn_all.items() if k in ('wq', 'wk', 'wv', 'wo', 'norm_w')}
    del _L1_xattn_all

    def _L2_xattn_setup():
        import jax, jax.numpy as jnp
        import numpy as np
        HEADS = 16
        HEAD_DIM = 64
        SUPPRESS = 20.0
        key = jax.random.key(seed)
        ks = jax.random.split(key, 8)
        B, HW, C, T, CT = (8, 2048, 512, 77, 1024)
        inner = HEADS * HEAD_DIM
        scale = 0.02
        return {'hidden_states': jax.random.normal(ks[0], (B, HW, C), jnp.float32), 'encoder_hidden_states': jax.random.normal(ks[1], (B, T, CT), jnp.float32), 'mask_A': (jax.random.uniform(ks[2], (HW,)) > 0.5).astype(jnp.float32), 'mask_B': (jax.random.uniform(ks[3], (HW,)) > 0.5).astype(jnp.float32), 'Wq': jax.random.normal(ks[4], (C, inner), jnp.float32) * scale, 'Wk': jax.random.normal(ks[5], (CT, inner), jnp.float32) * scale, 'Wv': jax.random.normal(ks[6], (CT, inner), jnp.float32) * scale, 'Wo': jax.random.normal(ks[7], (inner, C), jnp.float32) * scale, 'bo': jnp.zeros((C,), jnp.float32), 'token_indices_A': jnp.array([2, 3], dtype=jnp.int64), 'token_indices_B': jnp.array([5, 6], dtype=jnp.int64)}
    _L2_xattn_all = _L2_xattn_setup()
    _L2_xattn_in = {k: v for k, v in _L2_xattn_all.items() if k in ('Wq', 'Wk', 'Wv', 'Wo', 'bo', 'token_indices_A', 'token_indices_B')}
    del _L2_xattn_all

    def _L3_xattn_setup():
        import jax, jax.numpy as jnp
        import numpy as np
        D_MODEL = 512
        N_HEADS = 16
        N_KV_HEADS = 4
        HEAD_DIM = D_MODEL // N_HEADS
        SPEAKER_DIM = 1024
        EPS = 1e-05

        def rmsnorm(x, w, eps=EPS):
            xf = x.astype(jnp.float32)
            inv = jax.lax.rsqrt(jnp.mean(xf * xf, axis=-1, keepdims=True) + eps)
            return (xf * inv).astype(x.dtype) * w
        key = jax.random.key(seed)
        ks = jax.random.split(key, 7)
        B, T, S = (4, 1024, 256)
        x = jax.random.normal(ks[0], (B, T, D_MODEL), dtype=jnp.float32)
        cond = jax.random.normal(ks[1], (B, S, SPEAKER_DIM), dtype=jnp.float32)
        sq = 0.02
        wq = jax.random.normal(ks[2], (D_MODEL, N_HEADS * HEAD_DIM), dtype=jnp.float32) * sq
        wk = jax.random.normal(ks[3], (SPEAKER_DIM, N_KV_HEADS * HEAD_DIM), dtype=jnp.float32) * sq
        wv = jax.random.normal(ks[4], (SPEAKER_DIM, N_KV_HEADS * HEAD_DIM), dtype=jnp.float32) * sq
        wo = jax.random.normal(ks[5], (N_HEADS * HEAD_DIM, D_MODEL), dtype=jnp.float32) * sq
        norm_w = jnp.ones((D_MODEL,), dtype=jnp.float32)
        return {'x': x, 'cond': cond, 'wq': wq, 'wk': wk, 'wv': wv, 'wo': wo, 'norm_w': norm_w}
    _L3_xattn_all = _L3_xattn_setup()
    _L3_xattn_in = {k: v for k, v in _L3_xattn_all.items() if k in ('wq', 'wk', 'wv', 'wo', 'norm_w')}
    del _L3_xattn_all
    return {'x': x, 'ctx_2048': ctx_2048, 'mask_S_fk1': mask_S_fk1, 'mask_S_fk0': mask_S_fk0, 'L0_xattn_Wq': _L0_xattn_in['Wq'], 'L0_xattn_Wk': _L0_xattn_in['Wk'], 'L0_xattn_Wv': _L0_xattn_in['Wv'], 'L0_xattn_Wo': _L0_xattn_in['Wo'], 'L0_xattn_bo': _L0_xattn_in['bo'], 'L0_xattn_token_indices_A': _L0_xattn_in['token_indices_A'], 'L0_xattn_token_indices_B': _L0_xattn_in['token_indices_B'], 'L1_xattn_wq': _L1_xattn_in['wq'], 'L1_xattn_wk': _L1_xattn_in['wk'], 'L1_xattn_wv': _L1_xattn_in['wv'], 'L1_xattn_wo': _L1_xattn_in['wo'], 'L1_xattn_norm_w': _L1_xattn_in['norm_w'], 'L2_xattn_Wq': _L2_xattn_in['Wq'], 'L2_xattn_Wk': _L2_xattn_in['Wk'], 'L2_xattn_Wv': _L2_xattn_in['Wv'], 'L2_xattn_Wo': _L2_xattn_in['Wo'], 'L2_xattn_bo': _L2_xattn_in['bo'], 'L2_xattn_token_indices_A': _L2_xattn_in['token_indices_A'], 'L2_xattn_token_indices_B': _L2_xattn_in['token_indices_B'], 'L3_xattn_wq': _L3_xattn_in['wq'], 'L3_xattn_wk': _L3_xattn_in['wk'], 'L3_xattn_wv': _L3_xattn_in['wv'], 'L3_xattn_wo': _L3_xattn_in['wo'], 'L3_xattn_norm_w': _L3_xattn_in['norm_w']}

def reference(x, ctx_2048, mask_S_fk1, mask_S_fk0, L0_xattn_Wq, L0_xattn_Wk, L0_xattn_Wv, L0_xattn_Wo, L0_xattn_bo, L0_xattn_token_indices_A, L0_xattn_token_indices_B, L1_xattn_wq, L1_xattn_wk, L1_xattn_wv, L1_xattn_wo, L1_xattn_norm_w, L2_xattn_Wq, L2_xattn_Wk, L2_xattn_Wv, L2_xattn_Wo, L2_xattn_bo, L2_xattn_token_indices_A, L2_xattn_token_indices_B, L3_xattn_wq, L3_xattn_wk, L3_xattn_wv, L3_xattn_wo, L3_xattn_norm_w):
    import jax
    import jax.numpy as jnp

    def _L0_xattn_ref(hidden_states, encoder_hidden_states, mask_A, mask_B, Wq, Wk, Wv, Wo, bo, token_indices_A, token_indices_B):
        import jax, jax.numpy as jnp
        import numpy as np
        HEADS = 16
        HEAD_DIM = 64
        SUPPRESS = 20.0
        B, HW, C = hidden_states.shape
        T = encoder_hidden_states.shape[1]
        residual = hidden_states
        q = hidden_states @ Wq
        k = encoder_hidden_states @ Wk
        v = encoder_hidden_states @ Wv
        q = q.reshape(B, HW, HEADS, HEAD_DIM).transpose(0, 2, 1, 3)
        k = k.reshape(B, T, HEADS, HEAD_DIM).transpose(0, 2, 1, 3)
        v = v.reshape(B, T, HEADS, HEAD_DIM).transpose(0, 2, 1, 3)
        scale = HEAD_DIM ** (-0.5)
        logits = jnp.einsum('bhqd,bhkd->bhqk', q, k) * scale
        suppress_A_in = 1.0 - mask_A
        suppress_B_in = 1.0 - mask_B
        col_bias = jnp.zeros((HW, T), logits.dtype)
        col_bias = col_bias.at[:, token_indices_A].set((-SUPPRESS * suppress_A_in)[:, None])
        col_bias = col_bias.at[:, token_indices_B].set((-SUPPRESS * suppress_B_in)[:, None])
        logits = logits + col_bias[None, None, :, :]
        probs = jax.nn.softmax(logits, axis=-1)
        out = jnp.einsum('bhqk,bhkd->bhqd', probs, v)
        out = out.transpose(0, 2, 1, 3).reshape(B, HW, HEADS * HEAD_DIM)
        out = out @ Wo + bo
        out = out + residual
        return out

    def _L1_xattn_ref(x, cond, wq, wk, wv, wo, norm_w):
        import jax, jax.numpy as jnp
        import numpy as np
        D_MODEL = 512
        N_HEADS = 16
        N_KV_HEADS = 4
        HEAD_DIM = D_MODEL // N_HEADS
        SPEAKER_DIM = 1024
        EPS = 1e-05

        def rmsnorm(x, w, eps=EPS):
            xf = x.astype(jnp.float32)
            inv = jax.lax.rsqrt(jnp.mean(xf * xf, axis=-1, keepdims=True) + eps)
            return (xf * inv).astype(x.dtype) * w
        B, T, _ = x.shape
        S = cond.shape[1]
        n_rep = N_HEADS // N_KV_HEADS
        residual = x
        xn = rmsnorm(x, norm_w)
        q = (xn @ wq).reshape(B, T, N_HEADS, HEAD_DIM)
        k = (cond @ wk).reshape(B, S, N_KV_HEADS, HEAD_DIM)
        v = (cond @ wv).reshape(B, S, N_KV_HEADS, HEAD_DIM)
        qg = q.reshape(B, T, N_KV_HEADS, n_rep, HEAD_DIM)
        scale = 1.0 / np.sqrt(HEAD_DIM).astype(np.float32)
        scores = jnp.einsum('btgrd,bsgd->bgrts', qg, k) * scale
        attn = jax.nn.softmax(scores.astype(jnp.float32), axis=-1).astype(q.dtype)
        out = jnp.einsum('bgrts,bsgd->btgrd', attn, v).reshape(B, T, N_HEADS * HEAD_DIM)
        return residual + out @ wo

    def _L2_xattn_ref(hidden_states, encoder_hidden_states, mask_A, mask_B, Wq, Wk, Wv, Wo, bo, token_indices_A, token_indices_B):
        import jax, jax.numpy as jnp
        import numpy as np
        HEADS = 16
        HEAD_DIM = 64
        SUPPRESS = 20.0
        B, HW, C = hidden_states.shape
        T = encoder_hidden_states.shape[1]
        residual = hidden_states
        q = hidden_states @ Wq
        k = encoder_hidden_states @ Wk
        v = encoder_hidden_states @ Wv
        q = q.reshape(B, HW, HEADS, HEAD_DIM).transpose(0, 2, 1, 3)
        k = k.reshape(B, T, HEADS, HEAD_DIM).transpose(0, 2, 1, 3)
        v = v.reshape(B, T, HEADS, HEAD_DIM).transpose(0, 2, 1, 3)
        scale = HEAD_DIM ** (-0.5)
        logits = jnp.einsum('bhqd,bhkd->bhqk', q, k) * scale
        suppress_A_in = 1.0 - mask_A
        suppress_B_in = 1.0 - mask_B
        col_bias = jnp.zeros((HW, T), logits.dtype)
        col_bias = col_bias.at[:, token_indices_A].set((-SUPPRESS * suppress_A_in)[:, None])
        col_bias = col_bias.at[:, token_indices_B].set((-SUPPRESS * suppress_B_in)[:, None])
        logits = logits + col_bias[None, None, :, :]
        probs = jax.nn.softmax(logits, axis=-1)
        out = jnp.einsum('bhqk,bhkd->bhqd', probs, v)
        out = out.transpose(0, 2, 1, 3).reshape(B, HW, HEADS * HEAD_DIM)
        out = out @ Wo + bo
        out = out + residual
        return out

    def _L3_xattn_ref(x, cond, wq, wk, wv, wo, norm_w):
        import jax, jax.numpy as jnp
        import numpy as np
        D_MODEL = 512
        N_HEADS = 16
        N_KV_HEADS = 4
        HEAD_DIM = D_MODEL // N_HEADS
        SPEAKER_DIM = 1024
        EPS = 1e-05

        def rmsnorm(x, w, eps=EPS):
            xf = x.astype(jnp.float32)
            inv = jax.lax.rsqrt(jnp.mean(xf * xf, axis=-1, keepdims=True) + eps)
            return (xf * inv).astype(x.dtype) * w
        B, T, _ = x.shape
        S = cond.shape[1]
        n_rep = N_HEADS // N_KV_HEADS
        residual = x
        xn = rmsnorm(x, norm_w)
        q = (xn @ wq).reshape(B, T, N_HEADS, HEAD_DIM)
        k = (cond @ wk).reshape(B, S, N_KV_HEADS, HEAD_DIM)
        v = (cond @ wv).reshape(B, S, N_KV_HEADS, HEAD_DIM)
        qg = q.reshape(B, T, N_KV_HEADS, n_rep, HEAD_DIM)
        scale = 1.0 / np.sqrt(HEAD_DIM).astype(np.float32)
        scores = jnp.einsum('btgrd,bsgd->bgrts', qg, k) * scale
        attn = jax.nn.softmax(scores.astype(jnp.float32), axis=-1).astype(q.dtype)
        out = jnp.einsum('bgrts,bsgd->btgrd', attn, v).reshape(B, T, N_HEADS * HEAD_DIM)
        return residual + out @ wo
    x = _L0_xattn_ref(x, ctx_2048, mask_S_fk1, mask_S_fk0, L0_xattn_Wq, L0_xattn_Wk, L0_xattn_Wv, L0_xattn_Wo, L0_xattn_bo, L0_xattn_token_indices_A, L0_xattn_token_indices_B)
    x = _L1_xattn_ref(x, ctx_2048, L1_xattn_wq, L1_xattn_wk, L1_xattn_wv, L1_xattn_wo, L1_xattn_norm_w)
    x = _L2_xattn_ref(x, ctx_2048, mask_S_fk1, mask_S_fk0, L2_xattn_Wq, L2_xattn_Wk, L2_xattn_Wv, L2_xattn_Wo, L2_xattn_bo, L2_xattn_token_indices_A, L2_xattn_token_indices_B)
    x = _L3_xattn_ref(x, ctx_2048, L3_xattn_wq, L3_xattn_wk, L3_xattn_wv, L3_xattn_wo, L3_xattn_norm_w)
    return x

_drawn_inputs = setup_inputs


def setup_inputs(seed=0):
    import zlib

    import numpy as np

    out = dict(_drawn_inputs(seed))
    spreads = {'L0_xattn_bo': (0.0, 0.1),
     'L1_xattn_norm_w': (1.0, 0.6),
     'L2_xattn_bo': (0.0, 0.1),
     'L3_xattn_norm_w': (1.0, 0.6)}
    factors = {'mask_S_fk1': 8.0,
     'mask_S_fk0': 8.0,
     'L0_xattn_Wq': 2.781,
     'L0_xattn_Wk': 2.748,
     'L1_xattn_wq': 3.772,
     'L1_xattn_wk': 3.719,
     'L2_xattn_Wq': 2.685,
     'L3_xattn_wq': 3.782,
     'L3_xattn_wk': 3.756}
    for name, (base, spread) in spreads.items():
        noise = np.random.default_rng([zlib.crc32(name.encode()), seed]).standard_normal(out[name].shape)
        drawn = base * np.exp(spread * noise) if base else spread * noise
        out[name] = jnp.asarray(drawn.astype(out[name].dtype))
    for name, factor in factors.items():
        out[name] = (out[name] * factor).astype(out[name].dtype)
    return out
```

```python
from contextlib import ExitStack

import concourse.bass as bass
from concourse import mybir

F32 = mybir.dt.float32
F32R = mybir.dt.float32r
I32 = mybir.dt.int32
ALU = mybir.AluOpType
ACT = mybir.ActivationFunctionType
AX_X = mybir.AxisListType.X

P = 128
B, TOK, D = 8, 512, 512
CTX, CW = 77, 1024
ROWS = B * CTX
KC = CW // P
XC = D // P
PAIRS = 2
GROUPS, GH = 4, 4
TILES = TOK // P
SC = GH * CTX
CH = -(-SC // 3)
CHUNK_ROWS = [min(CH, SC - CH * n) for n in range(3)]
BLK = 256
HALF = ROWS // 2
SUPPRESS, EPS = 20.0, 1e-5
UNITS2 = 2 * GROUPS
VROWS = [min(P, ROWS - P * r) for r in range(-(-ROWS // P))]


class Kind:

    def __init__(self, name, heads_wide, kv_blocks, pieces, out_chunks):
        self.name = name
        self.Q = heads_wide
        self.blocks = kv_blocks
        self.pieces = pieces
        self.O = out_chunks
        self.DH = 128 * heads_wide // GH
        self.key_dmas = 2 if name == "A" else GH
        queries, acc = [], []
        for u in range(B * GROUPS):
            queries += [("q", u, m) for m in range(self.Q)]
            if name == "B" and u % GROUPS == 0:
                queries.append(("stats", u // GROUPS))
            acc += [("pv", u, m) for m in range(self.Q)]
            if u % GROUPS == GROUPS - 1:
                acc += [("proj", u // GROUPS, m) for m in range(XC)]
        self.at = {item: n for order in (queries, acc) for n, item in enumerate(order)}
        self.queries2, self.acc2 = len(queries) // (B // 2), len(acc) // (B // 2)


def value_pieces(width, outs):
    blocks, pieces = [], []
    for n in range(3):
        for h in range(GH):
            lo, hi = max(h * CTX, n * CH), min((h + 1) * CTX, n * CH + CHUNK_ROWS[n])
            if lo < hi:
                key = (n, h * outs // GH)
                if key not in blocks:
                    blocks.append(key)
                pieces.append((h, lo - h * CTX, hi - h * CTX, blocks.index(key), lo - n * CH))
    return blocks, pieces


KIND_A = Kind("A", 2, *value_pieces(64, 2), 8)
KIND_B = Kind("B", 1, *value_pieces(32, 1), 4)


def three_passes(pe, out, weights, moving, start, stop):
    pe.matmul(out, weights[0], moving[0], start=start, stop=False)
    pe.matmul(out, weights[0], moving[1], start=False, stop=False)
    return pe.matmul(out, weights[1], moving[0], start=False, stop=stop)


def wait_apart(eng, semaphore, value, seen):
    eng.wait_ge(semaphore, value)
    eng.sem_inc(seen, 1)


def context_block(nc, ctxT, kvw, k_scr, v_scr, k1_scr, v1_scr, x_in, stream):
    NJ = PAIRS * GROUPS
    with ExitStack() as ctx:
        def sb(name, shape, dt):
            return ctx.enter_context(nc.sbuf_tensor(name, shape, dt))

        def sem(name):
            return ctx.enter_context(nc.semaphore(name))

        ctx_raw = sb("ctx_raw", [P, KC, ROWS], F32)
        ctx_s = sb("ctx_s", [P, 2, KC, ROWS], F32R)
        w_raw = sb("kvw_raw", [P, 2, KC, BLK], F32)
        w_s = sb("kvw_s", [P, 2, 2, KC, BLK], F32R)
        k_out = sb("k_out", [P, 2, 2, ROWS], F32R)
        v_out = sb("v_out", [P, len(VROWS), 2, BLK], F32R)
        banks = [ctx.enter_context(nc.psum_tensor(f"ctx_bank{i}", [P, 512], F32)) for i in range(8)]

        ctx_loaded, w_loaded = sem("ctx_loaded"), [sem("kw_loaded"), sem("vw_loaded")]
        ctx_hi, ctx_lo = sem("ctx_hi"), sem("ctx_lo")
        w_hi, w_lo = [sem("kw_hi"), sem("vw_hi")], [sem("kw_lo"), sem("vw_lo")]
        k_mm, v_mm = sem("k_mm"), sem("v_mm")
        k_hi, k_lo, v_hi, v_lo = sem("k_hi"), sem("k_lo"), sem("v_hi"), sem("v_lo")
        k_stored, v_stored, x_copied = sem("k_stored"), sem("v_stored"), sem("x_copied")
        sp_seen = sem("ctx_sp_seen")
        NV = len(VROWS)
        FULL = sum(r == P for r in VROWS)

        block = ctx.enter_context(nc.Block())

        @block.sync
        def _(sp):
            for counted in (k_lo, v_lo, k_stored, v_stored):
                sp.sem_inc(counted, 1)
            sp.dma_start(ctx_raw[:, :, :], ctxT).then_inc(ctx_loaded, 16)
            for slot in range(2):
                sp.dma_start(w_raw[:, slot], kvw[slot]).then_inc(w_loaded[slot], 16)
            sp.dma_start(stream, x_in).then_inc(x_copied, 16)
            with sp.Fori(0, NJ) as j:
                for slot in range(2):
                    wait_apart(sp, w_hi[slot], j + 1, sp_seen)
                    wait_apart(sp, w_lo[slot], j + 1, sp_seen)
                    sp.dma_start(w_raw[:, slot], kvw[2 * j + 2 + slot]).then_inc(w_loaded[slot], 16)
                for m in range(2):
                    wait_apart(sp, k_lo, 4 * j + 2 * m + 3, sp_seen)
                    for h in range(2):
                        sp.dma_start(k_scr[j, :, :, m, h].rearrange("b q n -> q b n"),
                                     k_out[:, m, h].bitcast(F32).rearrange("q (b n) -> q b n", b=B))\
                          .then_inc(k_stored, 16)
                wait_apart(sp, v_lo, NV * j + NV + 1, sp_seen)
                sp.dma_start(v_scr[j, 0:FULL * P].rearrange("(r p) s n -> p r s n", p=P),
                             v_out[:, 0:FULL].bitcast(F32)).then_inc(v_stored, 16)
                sp.dma_start(v_scr[j, FULL * P:ROWS], v_out[0:VROWS[-1], FULL].bitcast(F32)).then_inc(v_stored, 16)
            for p in range(PAIRS):
                sp.wait_ge(k_lo, 4 * NJ + 2 * p + 3)
                for h in range(2):
                    sp.dma_start(k1_scr[p, :, :, h].rearrange("b q n -> q b n"),
                                 k_out[:, p, h].bitcast(F32).rearrange("q (b n) -> q b n", b=B))\
                      .then_inc(k_stored, 16)
                sp.wait_ge(v_lo, NV * (NJ + p + 1) + 1)
                for h in range(2):
                    sp.dma_start(v1_scr[p, 0:FULL * P, h].rearrange("(r p) n -> p r n", p=P),
                                 v_out[:, 0:FULL, h, 0:P].bitcast(F32)).then_inc(v_stored, 16)
                sp.dma_start(v1_scr[p, FULL * P:ROWS],
                             v_out[0:VROWS[-1], FULL, :, 0:P].bitcast(F32)).then_inc(v_stored, 16)
            sp.wait_ge(k_stored, 64 * NJ + 32 * PAIRS + 1)
            sp.wait_ge(v_stored, 32 * NJ + 48 * PAIRS + 1)
            sp.wait_ge(x_copied, 16)

        @block.scalar
        def _(act):
            def split_weights(slot, j):
                act.wait_ge(w_loaded[slot], 16 * j + 16)
                if slot == 0:
                    act.wait_ge(k_mm, 4 * j)
                else:
                    act.wait_ge(v_mm, NV * j)
                act.activation(w_s[:, slot, 0], w_raw[:, slot], ACT.Copy).then_inc(w_hi[slot], 1)

            def drain_keys(n, j, stored):
                m, h = n // 2, n % 2
                act.wait_ge(k_mm, 4 * j + n + 1)
                if n == 0:
                    act.wait_ge(k_stored, stored + 1)
                act.activation(k_out[:, m, 0, h * HALF:(h + 1) * HALF], banks[n][:, 0:HALF], ACT.Copy)\
                   .then_inc(k_hi, 1)

            def drain_values(r, item, width, stored):
                act.wait_ge(v_mm, item + 1)
                if r == 0:
                    act.wait_ge(v_stored, stored + 1)
                act.activation(v_out[0:VROWS[r], r, 0, 0:width], banks[4 + r % 4][0:VROWS[r], 0:width], ACT.Copy)\
                   .then_inc(v_hi, 1)

            act.wait_ge(ctx_loaded, 16)
            for k in range(KC):
                act.activation(ctx_s[:, 0, k], ctx_raw[:, k], ACT.Copy).then_inc(ctx_hi, 1)
            split_weights(0, 0)
            split_weights(1, 0)
            with act.Fori(0, NJ) as j:
                for n in range(4):
                    drain_keys(n, j, 64 * j)
                split_weights(0, j + 1)
                for r in range(NV):
                    drain_values(r, NV * j + r, BLK, 32 * j)
                split_weights(1, j + 1)
            for p in range(PAIRS):
                for h in range(2):
                    drain_keys(2 * p + h, NJ, 64 * NJ)
                for r in range(NV):
                    drain_values(r, NV * (NJ + p) + r, P, 32 * NJ + 48 * p)

        @block.vector
        def _(dve):
            def split_weights(slot, j):
                dve.wait_ge(w_hi[slot], j + 1)
                dve.tensor_tensor(w_s[:, slot, 1], w_raw[:, slot], w_s[:, slot, 0].bitcast(F32), ALU.subtract)\
                   .then_inc(w_lo[slot], 1)

            def drain_keys(n, j):
                m, h = n // 2, n % 2
                dve.wait_ge(k_hi, 4 * j + n + 1)
                dve.tensor_tensor(k_out[:, m, 1, h * HALF:(h + 1) * HALF], banks[n][:, 0:HALF],
                                  k_out[:, m, 0, h * HALF:(h + 1) * HALF].bitcast(F32), ALU.subtract)\
                   .then_inc(k_lo, 1)

            def drain_values(r, item, width):
                dve.wait_ge(v_hi, item + 1)
                dve.tensor_tensor(v_out[0:VROWS[r], r, 1, 0:width], banks[4 + r % 4][0:VROWS[r], 0:width],
                                  v_out[0:VROWS[r], r, 0, 0:width].bitcast(F32), ALU.subtract).then_inc(v_lo, 1)

            for k in range(KC):
                dve.wait_ge(ctx_hi, k + 1)
                dve.tensor_tensor(ctx_s[:, 1, k], ctx_raw[:, k], ctx_s[:, 0, k].bitcast(F32), ALU.subtract)\
                   .then_inc(ctx_lo, 1)
            split_weights(0, 0)
            split_weights(1, 0)
            with dve.Fori(0, NJ) as j:
                for n in range(4):
                    drain_keys(n, j)
                split_weights(0, j + 1)
                for r in range(NV):
                    drain_values(r, NV * j + r, BLK)
                split_weights(1, j + 1)
            for p in range(PAIRS):
                for h in range(2):
                    drain_keys(2 * p + h, NJ)
                for r in range(NV):
                    drain_values(r, NV * (NJ + p) + r, P)

        @block.tensor
        def _(pe):
            def keys(n, slot, col):
                h = n % 2
                for k in range(KC):
                    mm = three_passes(pe, banks[n][:, 0:HALF],
                                      [w_s[:, slot, s, k, col:col + P] for s in range(2)],
                                      [ctx_s[:, s, k, h * HALF:(h + 1) * HALF] for s in range(2)],
                                      k == 0, k == KC - 1)
                mm.then_inc(k_mm, 1)

            def values(r, slot, col, width):
                for k in range(KC):
                    mm = three_passes(pe, banks[4 + r % 4][0:VROWS[r], 0:width],
                                      [ctx_s[:, s, k, r * P:r * P + VROWS[r]] for s in range(2)],
                                      [w_s[:, slot, s, k, col:col + width] for s in range(2)],
                                      k == 0, k == KC - 1)
                mm.then_inc(v_mm, 1)

            pe.wait_ge(ctx_lo, KC)
            with pe.Fori(0, NJ) as j:
                pe.wait_ge(w_lo[0], j + 1)
                for n in range(4):
                    pe.wait_ge(k_lo, 4 * j + 1)
                    keys(n, 0, (n // 2) * P)
                pe.wait_ge(w_lo[1], j + 1)
                for r in range(NV):
                    pe.wait_ge(v_lo, NV * j + (2 if r == 4 else 1))
                    values(r, 1, 0, BLK)
            for p in range(PAIRS):
                pe.wait_ge(w_lo[p], NJ + 1)
                for h in range(2):
                    pe.wait_ge(k_lo, 4 * NJ + 1)
                    keys(2 * p + h, p, 0)
                for r in range(NV):
                    pe.wait_ge(v_lo, NV * (NJ + p) + (2 if r == 4 else 1))
                    values(r, p, P, P)


def attention_block(nc, stream, k_scr, v_scr, k1_scr, v1_scr, wqA, woA, wqB, woB, boA, normB, masks, tokens,
                    token_words):
    with ExitStack() as ctx:
        def sb(name, shape, dt):
            return ctx.enter_context(nc.sbuf_tensor(name, shape, dt))

        def sem(name):
            return ctx.enter_context(nc.semaphore(name))

        x = sb("x", [P, 2, XC, TOK], F32)
        x_s = sb("x_s", [P, 2, XC, TOK], F32R)
        q_s = sb("q_s", [P, 2, 2, 2, TOK], F32R)
        prob = sb("prob", [P, 2, TILES, SC], F32)
        pT_s = sb("pT_s", [P, 3, 2, TOK], F32R)
        o_s = sb("o_s", [P, 2, 8, TOK], F32R)
        w1 = sb("w1", [P, 2, 4096], F32R)
        w2 = sb("w2", [P, 2, 4096], F32R)
        stage = sb("stage", [P, 2048], F32)
        xsq = sb("xsq", [P, XC, TOK], F32)
        keys_s = sb("keys_s", [P, 2, 2 * SC], F32R)
        vals_s = sb("vals_s", [P, 2, 4, 2, P], F32R)
        ident = sb("ident", [P, P], F32)
        ones = sb("ones", [P, 1], F32)
        mhalf = sb("mhalf", [P, TILES], F32)
        mask_s = sb("mask_s", [P, TOK], F32R)
        hit_s = sb("hit_s", [P, PAIRS, SC], F32R)
        bo = sb("bo", [P, PAIRS, XC], F32)
        nw = sb("nw", [P, PAIRS, XC], F32)
        mx = sb("mx", [P, 2, 4 * GH], F32)
        sums = sb("sums", [P, 2, 4 * GH], F32)
        rinv = sb("rinv", [P, 2, 4 * GH], F32)
        ms = sb("ms", [P, 2, TILES], F32)
        rstd = sb("rstd", [P, 2, TILES], F32)
        hit_now = sb("hit_now", [P, SC], F32R)
        bo_now = sb("bo_now", [P, XC], F32)
        nw_now = sb("nw_now", [P, XC], F32)
        tok_i = sb("tok_i", [P, 8], I32)
        tok_f = sb("tok_f", [P, 2, 8], F32)
        mask_raw, mask_b = xsq[:, 0], xsq[:, 1]
        iota_t = xsq[:, 2, 0:CTX]
        cmp_t = [xsq[:, 2, CTX * (1 + n):CTX * (2 + n)] for n in range(4)]

        def bank(name):
            return ctx.enter_context(nc.psum_tensor(name, [P, 512], F32))

        q_bank = [bank("q_bank0"), bank("q_bank1")]
        s_bank = [bank("s_bank0"), bank("s_bank1")]
        t_bank = [bank("t_bank0"), bank("t_bank1")]
        acc_bank = [bank("acc_bank0"), bank("acc_bank1")]

        consts, cleared, setup_loaded = sem("consts"), sem("setup_cleared"), sem("setup_loaded")
        chain, setup_done, zeroed, picked = sem("dve_chain"), sem("setup_done"), sem("kv_zeroed"), sem("layer_picked")

        sp_seen, pool_seen = sem("sp_seen"), sem("pool_seen")

        class Sems:
            def __init__(self, k):
                self.all = []

                def named(name):
                    self.all.append(sem(f"{k}_{name}"))
                    return self.all[-1]
                self.w_loaded, self.w_scaled, self.w_hi, self.w_lo = map(named, ("w_loaded", "w_scaled", "w_hi", "w_lo"))
                self.x_loaded, self.x_hi, self.x_lo, self.x_sq = map(named, ("x_loaded", "x_hi", "x_lo", "x_sq"))
                self.keys_loaded = [named("keys_loaded0"), named("keys_loaded1")]
                self.vals_loaded = [named("vals_loaded0"), named("vals_loaded1")]
                self.q_mm, self.q_hi, self.q_out = map(named, ("q_mm", "q_hi", "q_out"))
                self.s_mm, self.s_max, self.s_sub = map(named, ("s_mm", "s_max", "s_sub"))
                self.p_exp, self.p_sum, self.p_inv, self.p_norm = map(named, ("p_exp", "p_sum", "p_inv", "p_norm"))
                self.t_mm, self.t_hi, self.t_lo = map(named, ("t_mm", "t_hi", "t_lo"))
                self.acc_mm, self.o_hi, self.acc_out = map(named, ("acc_mm", "o_hi", "acc_out"))
                self.rstd_ready = named("rstd_ready")
                self.stored = named("stored")

        sems = {"A": Sems("A"), "B": Sems("B")}
        NW = {"A": 4, "B": 2}

        def upto(J, per_unit, s, n):
            return J * (UNITS2 * per_unit) + (per_unit * s + n + 1)

        def acc_upto(kind, J, item):
            return J * kind.acc2 + (kind.at[item] + 2)

        def query_upto(kind, J, item):
            return J * kind.queries2 + (kind.at[item] + 2)

        def phase_start(eng, kind, p):
            if kind.name == "B":
                eng.wait_ge(sems["A"].stored, 16 * B * p + (16 * B + 1))
            else:
                eng.wait_ge(sems["B"].stored, 16 * B * p + 1)

        def pipeline(eng, p, first, step):
            first()
            step(4 * p, 0, False)
            with eng.Fori(0, B // 2 - 1) as it:
                J = 4 * p + it
                for s in range(1, UNITS2 + 1):
                    step(J, s, False)
            for s in range(1, UNITS2 + 1):
                step(4 * p + (B // 2 - 1), s, True)

        def exists(s, ends):
            return s < UNITS2 or not ends

        block = ctx.enter_context(nc.Block())

        @block.sync
        def _(sp):
            for S in sems.values():
                for counted in S.all:
                    sp.sem_inc(counted, 1)
            sp.wait_ge(cleared, 1)
            sp.dma_start(mask_raw[0:1], masks[0:1]).then_inc(setup_loaded, 16)
            sp.dma_start(mask_raw[32:33], masks[0:1]).then_inc(setup_loaded, 16)
            sp.dma_start(mask_raw[64:65], masks[1:2]).then_inc(setup_loaded, 16)
            sp.dma_start(mask_raw[96:97], masks[1:2]).then_inc(setup_loaded, 16)
            sp.dma_start(tok_i[:, :], tokens[:, ::token_words].partition_broadcast(P)).then_inc(setup_loaded, 16)
            sp.dma_start(bo[:, :, :], boA).then_inc(setup_loaded, 16)
            sp.dma_start(nw[:, :, :], normB).then_inc(setup_loaded, 16)

            def layer(kind, p):
                S = sems[kind.name]

                def load_x(b, slot):
                    sp.dma_start(x[:, slot], stream[b]).then_inc(S.x_loaded, 16)

                def load_keys(J, s, b):
                    g, slot = s % GROUPS, s % 2
                    if kind.name == "A":
                        keys = keys_s[:, slot].bitcast(F32).rearrange("q (c n) -> q c n", c=4)
                        for e in range(2):
                            sp.dma_start(keys[64 * e:64 * e + 64, :, CTX * e:CTX * e + CTX],
                                         k_scr[4 * p + g, b, 64 * e:64 * e + 64].rearrange("q c h n -> q (c h) n"))\
                              .then_inc(S.keys_loaded[slot], 16)
                    else:
                        keys = keys_s[:, slot].bitcast(F32).rearrange("q (h n) -> q h n", h=2)
                        for r in range(GH):
                            sp.dma_start(keys[32 * r:32 * r + 32, :, CTX * r:CTX * r + CTX],
                                         k1_scr[p, b, 32 * g:32 * g + 32]).then_inc(S.keys_loaded[slot], 16)

                def load_vals(J, s, b):
                    g, slot, w = s % GROUPS, s % 2, kind.DH
                    vals = vals_s[:, slot].bitcast(F32)
                    for h, t0, t1, blk, row in kind.pieces:
                        src = (v_scr[4 * p + g, b, t0:t1, :, w * h:w * h + w] if kind.name == "A"
                               else v1_scr[p, b, t0:t1, :, w * g:w * g + w])
                        col = w * h % P
                        sp.dma_start(vals[row:row + t1 - t0, blk, :, col:col + w], src)\
                          .then_inc(S.vals_loaded[slot], 16)

                def step(J, s, it, ends):
                    if exists(s + 2, ends):
                        wait_apart(sp, S.s_mm, upto(J, TILES, s, TILES), sp_seen)
                        load_keys(J, s + 2, 2 * it + (s + 2) // GROUPS)
                    if s >= 1 and exists(s + 1, ends):
                        wait_apart(sp, S.acc_mm, acc_upto(kind, J, ("pv", s - 1, kind.Q - 1)), sp_seen)
                        load_vals(J, s + 1, 2 * it + (s + 1) // GROUPS)
                    if s % GROUPS == 0 and s >= 1:
                        b = s // GROUPS - 1
                        wait_apart(sp, S.acc_out, acc_upto(kind, J, ("proj", b, XC - 1)), sp_seen)
                        sp.dma_start(stream[2 * it + b], x[:, b % 2]).then_inc(S.stored, 16)
                        wait_apart(sp, S.stored, 32 * J + (16 * (b + 1) + 1), sp_seen)

                for c in range(NW[kind.name]):
                    if c == 0:
                        phase_start(sp, kind, p)
                        sp.sem_inc(sp_seen, 1)
                    else:
                        wait_apart(sp, S.w_lo, NW[kind.name] * p + (c + 1), sp_seen)
                    if kind.name == "A":
                        src = wqA[p, c] if c < 2 else woA[p, c - 2]
                    else:
                        src = wqB[p] if c == 0 else woB[p]
                    sp.dma_start(stage[:, :], src).then_inc(S.w_loaded, 16)
                load_x(0, 0)
                wait_apart(sp, zeroed, 4 * p + (2 if kind.name == "A" else 4), sp_seen)
                for s in range(2):
                    load_keys(4 * p, s, 0)
                    load_vals(4 * p, s, 0)
                step(4 * p, 0, 0, False)
                wait_apart(sp, S.x_loaded, 128 * p + 17, sp_seen)
                load_x(1, 1)
                with sp.Fori(0, B // 2 - 1) as it:
                    J = 4 * p + it
                    for s in range(1, UNITS2 + 1):
                        step(J, s, it, False)
                        if s % GROUPS == 0:
                            b = s // GROUPS + 1
                            wait_apart(sp, S.x_loaded, 32 * J + (16 * b + 1), sp_seen)
                            load_x(2 * it + b, b % 2)
                last = B // 2 - 1
                for s in range(1, UNITS2 + 1):
                    step(4 * p + last, s, last, True)

            with sp.Fori(0, PAIRS) as p:
                layer(KIND_A, p)
                layer(KIND_B, p)

        @block.tensor
        def _(pe):
            def layer(kind, p):
                S = sems[kind.name]
                Q, a = kind.Q, kind.name == "A"
                if a:
                    wq = [w1[:, s, :].rearrange("q (k n) -> q k n", k=XC) for s in range(2)]
                    wo = [w2[:, s, :].rearrange("q (k n) -> q k n", k=8) for s in range(2)]
                else:
                    wq = [w1[:, s, 0:2048].rearrange("q (k n) -> q k n", k=XC) for s in range(2)]
                    wo = [w1[:, s, 2048:4096].rearrange("q (k n) -> q k n", k=XC) for s in range(2)]

                def scores(J, s, t):
                    slot = s % 2
                    if t == 0:
                        pe.wait_ge(S.q_out, query_upto(kind, J, ("q", s, Q - 1)))
                        pe.wait_ge(S.keys_loaded[slot], (J * 4 + (s // 2 + 1)) * (16 * kind.key_dmas) + 1)
                    if 4 * s + t >= 2:
                        pe.wait_ge(S.s_sub, upto(J, TILES, s, t - 1))
                    out = s_bank[t % 2]
                    tok = slice(t * P, t * P + P)
                    if a:
                        pe.matmul(out[:, 0:SC], mask_s[:, tok], hit_now[:, :], start=True, stop=False)
                        keys = keys_s[:, slot].rearrange("q (c h n) -> q c h n", c=2, h=2)
                        for c in range(2):
                            mm = three_passes(pe, out[:, 2 * CTX * c:2 * CTX * (c + 1)],
                                              [q_s[:, slot, h, c, tok] for h in range(2)],
                                              [keys[:, c, h] for h in range(2)], False, c == 1)
                    else:
                        keys = keys_s[:, slot].rearrange("q (h n) -> q h n", h=2)
                        mm = three_passes(pe, out[:, 0:SC], [q_s[:, slot, h, 0, tok] for h in range(2)],
                                          [keys[:, h] for h in range(2)], True, True)
                    mm.then_inc(S.s_mm, 1)

                def queries(J, s, m, chunks):
                    item = kind.at[("q", s, m)]
                    if 0 in chunks and item >= 2:
                        pe.wait_ge(S.q_out, J * kind.queries2 + item)
                    col = (s % GROUPS * Q + m) * P
                    for k in chunks:
                        if s % GROUPS == 0 and m == 0:
                            pe.wait_ge(S.x_lo, 8 * J + (4 * (s // GROUPS) + k + 2))
                        mm = three_passes(pe, q_bank[item % 2][:, :], [w[:, k, col:col + P] for w in wq],
                                          [x_s[:, h, k] for h in range(2)], k == 0, k == XC - 1)
                    if XC - 1 in chunks:
                        mm.then_inc(S.q_mm, 1)

                def turn(J, s, n):
                    if n == 0:
                        pe.wait_ge(S.p_norm, upto(J, 1, s, 1))
                    pe.wait_ge(S.t_lo, upto(J, 3, s, n - 1 if 3 * s + n >= 1 else 0))
                    rows = CHUNK_ROWS[n]
                    for t in range(TILES):
                        mm = pe.transpose(t_bank[(3 * s + n) % 2][0:rows, t * P:t * P + P],
                                          prob[:, s % 2, t, CH * n:CH * n + rows], ident[:, :])
                    mm.then_inc(S.t_mm, 1)

                def acc_free(J, item):
                    n = kind.at[item]
                    pe.wait_ge(S.acc_out, J * kind.acc2 + max(n, 1))
                    return acc_bank[n % 2]

                def values(J, s, m):
                    out = acc_free(J, ("pv", s, m))
                    if m == 0:
                        pe.wait_ge(S.vals_loaded[s % 2], (J * 4 + (s // 2 + 1)) * (16 * len(kind.pieces)) + 1)
                    mine = [i for i, (_, o) in enumerate(kind.blocks) if o == m]
                    for i in mine:
                        n = kind.blocks[i][0]
                        rows = CHUNK_ROWS[n]
                        pe.wait_ge(S.t_lo, upto(J, 3, s, n + 1))
                        mm = three_passes(pe, out[:, :], [vals_s[0:rows, s % 2, i, h] for h in range(2)],
                                          [pT_s[0:rows, n, h] for h in range(2)], i == mine[0], i == mine[-1])
                    mm.then_inc(S.acc_mm, 1)

                def project(J, b, m):
                    out = acc_free(J, ("proj", b, m))
                    if m == 0:
                        pe.wait_ge(S.acc_out, acc_upto(kind, J, ("pv", GROUPS * b + GROUPS - 1, Q - 1)))
                    for k in range(kind.O):
                        mm = three_passes(pe, out[:, :], [w[:, k, m * P:m * P + P] for w in wo],
                                          [o_s[:, h, k] for h in range(2)], k == 0, k == kind.O - 1)
                    mm.then_inc(S.acc_mm, 1)

                def stats(J, b):
                    item = kind.at[("stats", b)]
                    out = q_bank[item % 2]
                    pe.wait_ge(S.q_out, J * kind.queries2 + item)
                    pe.wait_ge(S.x_sq, 8 * J + (4 * (b + 1) + 1))
                    for t in range(TILES):
                        for k in range(XC):
                            mm = pe.matmul(out[:, t:t + 1], xsq[:, k, t * P:t * P + P], ones[:, :],
                                           start=(t == 0 and k == 0), stop=(t == TILES - 1 and k == XC - 1),
                                           skip_group_check=True)
                    mm.then_inc(S.q_mm, 1)

                def first():
                    pe.wait_ge(S.w_lo, NW[kind.name] * p + (NW[kind.name] + 1))
                    for m in range(Q):
                        queries(4 * p, 0, m, range(XC))
                    if not a:
                        stats(4 * p, 0)

                def step(J, s, ends):
                    live, has_next, has_last = exists(s, ends), exists(s + 1, ends), s >= 1
                    if live:
                        scores(J, s, 0)
                        scores(J, s, 1)
                    if has_next:
                        queries(J, s + 1, 0, range(XC) if a else range(2))
                    if live:
                        scores(J, s, 2)
                        scores(J, s, 3)
                    if has_last:
                        turn(J, s - 1, 0)
                        turn(J, s - 1, 1)
                    if has_next:
                        queries(J, s + 1, Q - 1, range(XC) if a else range(2, XC))
                    if not a and s % GROUPS == GROUPS - 1 and has_next:
                        stats(J, (s + 1) // GROUPS)
                    if has_last:
                        turn(J, s - 1, 2)
                        for m in range(Q):
                            values(J, s - 1, m)
                    if has_last and s % GROUPS == 0:
                        for m in range(XC):
                            project(J, s // GROUPS - 1, m)

                pipeline(pe, p, first, step)

            pe.wait_ge(consts, 4)
            pe.wait_ge(setup_done, 1)
            with pe.Fori(0, PAIRS) as p:
                layer(KIND_A, p)
                layer(KIND_B, p)

        @block.scalar
        def _(act):
            def layer(kind, p):
                S = sems[kind.name]
                Q, a = kind.Q, kind.name == "A"

                def split_x(J, b):
                    for k in range(XC):
                        if k == 0:
                            act.wait_ge(S.x_loaded, 32 * J + (16 * (b + 1) + 1))
                        act.activation(x_s[:, 0, k], x[:, b % 2, k], ACT.Copy).then_inc(S.x_hi, 1)
                    if not a:
                        if b >= 1:
                            act.wait_ge(S.q_mm, query_upto(kind, J, ("stats", b - 1)))
                        for k in range(XC):
                            act.activation(xsq[:, k], x[:, b % 2, k], ACT.Square).then_inc(S.x_sq, 1)

                def exps(J, s, half):
                    tiles = range(2 * half, 2 * half + 2)
                    if a:
                        act.wait_ge(S.s_sub, upto(J, TILES, s, 2 * half + 2))
                        act.activation(prob[:, s % 2, 2 * half:2 * half + 2], prob[:, s % 2, 2 * half:2 * half + 2],
                                       ACT.Exp, scale=float(kind.DH) ** -0.5).then_inc(S.p_exp, 1)
                        return
                    if half == 0:
                        act.wait_ge(S.rstd_ready, 2 * J + (s // GROUPS + 2))
                    for t in tiles:
                        act.wait_ge(S.s_sub, upto(J, TILES, s, t + 1))
                        e = act.activation(prob[:, s % 2, t], prob[:, s % 2, t], ACT.Exp,
                                           scale=rstd[:, s // GROUPS % 2, t:t + 1])
                    e.then_inc(S.p_exp, 1)

                def q_hi(J, s, m):
                    act.wait_ge(S.q_mm, query_upto(kind, J, ("q", s, m)))
                    if m == 0 and s >= 1:
                        act.wait_ge(S.s_mm, upto(J, TILES, s - 1, 0))
                    act.activation(q_s[:, s % 2, 0, m], q_bank[kind.at[("q", s, m)] % 2][:, :], ACT.Copy).then_inc(S.q_hi, 1)

                def t_hi(J, s, n):
                    act.wait_ge(S.t_mm, upto(J, 3, s, n + 1))
                    if n == 0:
                        act.wait_ge(S.acc_mm, J * kind.acc2 + (kind.at[("pv", s, 0)] + 1))
                    rows = CHUNK_ROWS[n]
                    act.activation(pT_s[0:rows, n, 0], t_bank[(3 * s + n) % 2][0:rows, :], ACT.Copy)\
                       .then_inc(S.t_hi, 1)

                def o_hi(J, s, m):
                    item = ("pv", s, m)
                    act.wait_ge(S.acc_mm, acc_upto(kind, J, item))
                    act.activation(o_s[:, 0, s % GROUPS * Q + m], acc_bank[kind.at[item] % 2][:, :], ACT.Copy)\
                       .then_inc(S.o_hi, 1)

                def first():
                    phase_start(act, kind, p)
                    for c in range(NW[kind.name]):
                        act.wait_ge(S.w_loaded, (NW[kind.name] * p + (c + 1)) * 16 + 1)
                        if not a and c == 0:
                            act.wait_ge(S.w_scaled, p + 2)
                        dst = (w1 if c < 2 else w2)[:, 0, 2048 * (c % 2):2048 * (c % 2) + 2048]
                        act.activation(dst, stage[:, :], ACT.Copy).then_inc(S.w_hi, 1)
                    split_x(4 * p, 0)
                    for m in range(Q):
                        q_hi(4 * p, 0, m)

                def step(J, s, ends):
                    live, has_next, has_last = exists(s, ends), exists(s + 1, ends), s >= 1
                    if live:
                        exps(J, s, 0)
                    if has_next and a:
                        q_hi(J, s + 1, 0)
                    if live:
                        exps(J, s, 1)
                    if has_last:
                        t_hi(J, s - 1, 0)
                        t_hi(J, s - 1, 1)
                    if has_next:
                        q_hi(J, s + 1, Q - 1)
                    if has_last:
                        t_hi(J, s - 1, 2)
                        for m in range(Q):
                            o_hi(J, s - 1, m)
                    if s % GROUPS == 2 and exists(s + 2, ends):
                        split_x(J, s // GROUPS + 1)

                pipeline(act, p, first, step)

            with act.Fori(0, PAIRS) as p:
                layer(KIND_A, p)
                layer(KIND_B, p)

        @block.vector
        def _(dve):
            links = [0]

            def link(ins):
                links[0] += 1
                ins.then_inc(chain, 1)
                dve.wait_ge(chain, links[0])

            link(dve.memset(hit_s[:, :, :].bitcast(F32), 0.0))
            dve.wait_ge(consts, 5)
            dve.wait_ge(setup_loaded, 16 * 7)
            link(dve.tensor_scalar(mask_b, mask_raw, 1.0, SUPPRESS * float(KIND_A.DH) ** 0.5, ALU.subtract, ALU.mult))
            link(dve.tensor_copy(mask_s[:, :], mask_b))
            for row in (32, 96):
                link(dve.tensor_tensor(mask_s[row:row + 1, :], mask_b[row:row + 1], mask_s[row:row + 1, :].bitcast(F32),
                                       ALU.subtract))
            link(dve.tensor_copy(tok_f[:, 0, :], tok_i[:, :]))
            link(dve.tensor_scalar(tok_f[:, 1, :], tok_f[:, 0, :], float(CTX), None, ALU.add))
            for p in range(PAIRS):
                for which in range(2):
                    hits = [(w, 4 * p + 2 * which + i) for w in range(2) for i in range(2)]
                    for n, (w, i) in enumerate(hits):
                        if n == 0:
                            link(dve.tensor_scalar(cmp_t[which], iota_t, tok_f[:, w, i:i + 1], None, ALU.is_equal))
                        else:
                            link(dve.scalar_tensor_tensor(out=cmp_t[which], in0=iota_t, scalar=tok_f[:, w, i:i + 1],
                                                          in1=cmp_t[which], op0=ALU.is_equal, op1=ALU.max))
                link(dve.tensor_tensor(cmp_t[2], cmp_t[0], cmp_t[1], ALU.mult))
                link(dve.tensor_tensor(cmp_t[0], cmp_t[0], cmp_t[2], ALU.subtract))
                for row in (0, 32, 64, 96):
                    link(dve.tensor_copy(hit_s[row:row + 1, p].rearrange("q (h n) -> q h n", h=GH),
                                         cmp_t[row // 64][row:row + 1].unsqueeze(1).broadcast_to([1, GH, CTX])))
            dve.memset(bo_now[:, :], 0.0).then_inc(setup_done, 1)
            dve.wait_ge(setup_done, 1)

            def layer(kind, p):
                S = sems[kind.name]
                Q, a = kind.Q, kind.name == "A"

                def halves(J, s, half):
                    slot = s % 2
                    for t in (2 * half, 2 * half + 1):
                        dve.wait_ge(S.s_mm, upto(J, TILES, s, t + 1))
                        dve.tensor_reduce(mx[:, slot, GH * t:GH * t + GH],
                                          s_bank[t % 2][:, 0:SC].rearrange("q (h n) -> q h n", h=GH),
                                          AX_X, ALU.max).then_inc(S.s_max, 1)
                    for t in (2 * half, 2 * half + 1):
                        if t == 0 and s >= 1:
                            dve.wait_ge(S.t_mm, upto(J, 3, s - 1, 0))
                        dve.wait_ge(S.s_max, upto(J, TILES, s, t + 1))
                        dve.tensor_tensor(prob[:, slot, t].rearrange("q (h n) -> q h n", h=GH),
                                          s_bank[t % 2][:, 0:SC].rearrange("q (h n) -> q h n", h=GH),
                                          mx[:, slot, GH * t:GH * t + GH].unsqueeze(2).broadcast_to([P, GH, CTX]),
                                          ALU.subtract).then_inc(S.s_sub, 1)

                def q_lo(J, s, m):
                    dve.wait_ge(S.q_hi, upto(J, Q, s, m + 1))
                    dve.tensor_tensor(q_s[:, s % 2, 1, m], q_bank[kind.at[("q", s, m)] % 2][:, :],
                                      q_s[:, s % 2, 0, m].bitcast(F32), ALU.subtract).then_inc(S.q_out, 1)

                def t_lo(J, s, n):
                    rows = CHUNK_ROWS[n]
                    dve.wait_ge(S.t_hi, upto(J, 3, s, n + 1))
                    dve.tensor_tensor(pT_s[0:rows, n, 1], t_bank[(3 * s + n) % 2][0:rows, :],
                                      pT_s[0:rows, n, 0].bitcast(F32), ALU.subtract).then_inc(S.t_lo, 1)

                def o_lo(J, s, m):
                    c = s % GROUPS * Q + m
                    dve.wait_ge(S.o_hi, upto(J, Q, s, m + 1))
                    dve.tensor_tensor(o_s[:, 1, c], acc_bank[kind.at[("pv", s, m)] % 2][:, :],
                                      o_s[:, 0, c].bitcast(F32), ALU.subtract).then_inc(S.acc_out, 1)

                def denominators(J, s):
                    slot = s % 2
                    dve.wait_ge(S.p_exp, upto(J, 2, s, 2))
                    dve.tensor_reduce(sums[:, slot], prob[:, slot].rearrange("q t (h n) -> q (t h) n", h=GH),
                                      AX_X, ALU.add).then_inc(S.p_sum, 1)
                    dve.wait_ge(S.p_sum, upto(J, 1, s, 1))
                    dve.reciprocal(rinv[:, slot], sums[:, slot]).then_inc(S.p_inv, 1)

                def mean_squares(J, b):
                    item = ("stats", b)
                    dve.wait_ge(S.q_mm, query_upto(kind, J, item))
                    dve.tensor_scalar(ms[:, b % 2], q_bank[kind.at[item] % 2][:, 0:TILES], kind.DH / D,
                                      EPS * kind.DH, ALU.mult, ALU.add).then_inc(S.q_out, 1)

                def add_result(J, b, m):
                    item = ("proj", b, m)
                    dve.wait_ge(S.acc_mm, acc_upto(kind, J, item))
                    out = acc_bank[kind.at[item] % 2][:, :]
                    if a:
                        dve.scalar_tensor_tensor(out=x[:, b % 2, m], in0=out, scalar=bo_now[:, m:m + 1],
                                                 in1=x[:, b % 2, m], op0=ALU.add, op1=ALU.add).then_inc(S.acc_out, 1)
                    else:
                        dve.tensor_tensor(x[:, b % 2, m], out, x[:, b % 2, m], ALU.add).then_inc(S.acc_out, 1)

                def first():
                    phase_start(dve, kind, p)
                    if a:
                        dve.tensor_copy(hit_now[:, :], hit_s[:, p].bitcast(F32)).then_inc(picked, 1)
                        dve.tensor_copy(bo_now[:, :], bo[:, p]).then_inc(picked, 1)
                        dve.tensor_copy(nw_now[:, :], nw[:, p]).then_inc(picked, 1)
                        dve.wait_ge(picked, 3 * p + 3)
                    for c in range(NW[kind.name]):
                        if not a and c == 0:
                            dve.wait_ge(S.w_loaded, 32 * p + 17)
                            for k in range(XC):
                                sc = dve.tensor_scalar(stage[:, 512 * k:512 * k + 512], stage[:, 512 * k:512 * k + 512],
                                                       nw_now[:, k:k + 1], None, ALU.mult)
                            sc.then_inc(S.w_scaled, 1)
                        dve.wait_ge(S.w_hi, NW[kind.name] * p + (c + 2))
                        w, part = (w1 if c < 2 else w2), slice(2048 * (c % 2), 2048 * (c % 2) + 2048)
                        dve.tensor_tensor(w[:, 1, part], stage[:, :], w[:, 0, part].bitcast(F32), ALU.subtract)                           .then_inc(S.w_lo, 1)
                    for m in range(Q):
                        q_lo(4 * p, 0, m)
                    if not a:
                        mean_squares(4 * p, 0)

                def step(J, s, ends):
                    live, has_next, has_last = exists(s, ends), exists(s + 1, ends), s >= 1
                    if live:
                        halves(J, s, 0)
                    if has_next and a:
                        q_lo(J, s + 1, 0)
                    if live:
                        halves(J, s, 1)
                    if has_last:
                        t_lo(J, s - 1, 0)
                        t_lo(J, s - 1, 1)
                    if has_next:
                        q_lo(J, s + 1, Q - 1)
                    if not a and s % GROUPS == GROUPS - 1 and has_next:
                        mean_squares(J, (s + 1) // GROUPS)
                    if has_last:
                        t_lo(J, s - 1, 2)
                        for m in range(Q):
                            o_lo(J, s - 1, m)
                    if live:
                        denominators(J, s)
                    if has_last and s % GROUPS == 0:
                        for m in range(XC):
                            add_result(J, s // GROUPS - 1, m)

                pipeline(dve, p, first, step)

            with dve.Fori(0, PAIRS) as p:
                layer(KIND_A, p)
                layer(KIND_B, p)

        @block.gpsimd
        def _(pool):
            pool.memset(xsq[:, :, :], 0.0).then_inc(cleared, 1)
            pool.memset(ident[:, :], 0.0).then_inc(consts, 1)
            pool.memset(ones[:, :], 1.0).then_inc(consts, 1)
            pool.memset(mhalf[:, :], -0.5).then_inc(consts, 1)
            pool.wait_ge(consts, 3)
            pool.wait_ge(cleared, 1)
            pool.affine_select(out=ident[:, :], in_=ident[:, :], compare_op=ALU.not_equal, fill=1.0, base=0,
                               pattern=[[-1, P]], channel_multiplier=1).then_inc(consts, 1)
            pool.iota(iota_t, [[1, CTX]], base=0, channel_multiplier=0,
                      allow_small_or_imprecise_dtypes=True).then_inc(consts, 1)

            def layer(kind, p):
                S = sems[kind.name]
                a = kind.name == "A"

                def x_lo(J, b):
                    for k in range(XC):
                        pool.wait_ge(S.x_hi, 8 * J + (4 * b + k + 2))
                        pool.tensor_tensor(x_s[:, 1, k], x[:, b % 2, k], x_s[:, 0, k].bitcast(F32), ALU.subtract)                            .then_inc(S.x_lo, 1)

                def normalise(J, s):
                    slot = s % 2
                    pool.wait_ge(S.p_inv, upto(J, 1, s, 1))
                    view = prob[:, slot].rearrange("q t (h n) -> q (t h) n", h=GH)
                    pool.tensor_tensor(view, view, rinv[:, slot].unsqueeze(2).broadcast_to([P, TILES * GH, CTX]),
                                       ALU.mult).then_inc(S.p_norm, 1)

                def root(J, b):
                    pool.wait_ge(S.q_out, query_upto(kind, J, ("stats", b)))
                    pool.tensor_tensor(rstd[:, b % 2], ms[:, b % 2], mhalf[:, :], ALU.pow).then_inc(S.rstd_ready, 1)

                phase_start(pool, kind, p)
                pool.sem_inc(pool_seen, 1)
                pool.memset(keys_s[:, :, :].bitcast(F32), 0.0).then_inc(zeroed, 1)
                pool.memset(vals_s[:, :, :, :, :].bitcast(F32), 0.0).then_inc(zeroed, 1)

                def first():
                    x_lo(4 * p, 0)
                    if not a:
                        root(4 * p, 0)

                def step(J, s, ends):
                    if s % GROUPS == 2 and exists(s + 2, ends):
                        x_lo(J, s // GROUPS + 1)
                    if exists(s, ends):
                        normalise(J, s)
                    if not a and s % GROUPS == GROUPS - 1 and exists(s + 1, ends):
                        root(J, (s + 1) // GROUPS)

                pipeline(pool, p, first, step)

            with pool.Fori(0, PAIRS) as p:
                layer(KIND_A, p)
                layer(KIND_B, p)


def build(nc, words):
    def dram(name, shape, dt=F32, kind="ExternalInput"):
        return nc.dram_tensor(name, shape, dt, kind=kind).ap()

    x_in = dram("x_in", (B, P, XC, TOK))
    ctxT = dram("ctxT", (P, KC, ROWS))
    kvw = dram("kvw", (2 * PAIRS * GROUPS + 2, P, KC, BLK))
    wqA, woA = dram("wqA", (PAIRS, 2, P, 2048)), dram("woA", (PAIRS, 2, P, 2048))
    wqB, woB = dram("wqB", (PAIRS, P, 2048)), dram("woB", (PAIRS, P, 2048))
    boA, normB = dram("boA", (P, PAIRS, XC)), dram("normB", (P, PAIRS, XC))
    masks, tokens = dram("masks", (2, TOK)), dram("tokens", (1, 8 * words), I32)
    stream = dram("stream", (B, P, XC, TOK), kind="ExternalOutput")
    k_scr = dram("k_scr", (PAIRS * GROUPS, B, P, 2, 2, CTX), kind="Internal")
    v_scr = dram("v_scr", (PAIRS * GROUPS, ROWS, 2, BLK), kind="Internal")
    k1_scr = dram("k1_scr", (PAIRS, B, P, 2, CTX), kind="Internal")
    v1_scr = dram("v1_scr", (PAIRS, ROWS, 2, P), kind="Internal")
    context_block(nc, ctxT, kvw, k_scr, v_scr, k1_scr, v1_scr, x_in, stream)
    attention_block(nc, stream,
                    k_scr,
                    v_scr.rearrange("j (b t) s n -> j b t s n", b=B),
                    k1_scr,
                    v1_scr.rearrange("j (b t) s n -> j b t s n", b=B),
                    wqA, woA, wqB, woB, boA, normB, masks, tokens, words)


def kernel(**inputs):
    import numpy as np
    import concourse.bacc as bacc
    from concourse.bass_utils import run_bass_kernel_spmd as run

    def arr(name):
        return np.asarray(inputs[name])

    def by_channel(w, chunks):
        return w.reshape(chunks, P, -1).transpose(1, 0, 2)

    def blocks(w):
        return by_channel(w, KC).reshape(P, KC, -1, BLK).transpose(2, 0, 1, 3)

    kvw = []
    for l in ("L0", "L2"):
        k, v = blocks(arr(l + "_xattn_Wk")), blocks(arr(l + "_xattn_Wv"))
        for g in range(GROUPS):
            kvw += [k[g], v[g]]
    for l in ("L1", "L3"):
        kvw.append(blocks(np.concatenate([arr(l + "_xattn_wk"), arr(l + "_xattn_wv")], axis=1))[0])
    two = lambda name, pair: np.stack([arr(f"{l}_xattn_{name}") for l in pair])
    A, BB = ("L0", "L2"), ("L1", "L3")
    halves = lambda w, c: np.stack([by_channel(m, c).reshape(P, 2, 2048).transpose(1, 0, 2) for m in w])
    tokens = np.concatenate([arr(f"{l}_xattn_token_indices_{w}") for l in A for w in "AB"])
    words = tokens.dtype.itemsize // 4
    maps = {
        "x_in": arr("x").transpose(0, 2, 1).reshape(B, XC, P, TOK).transpose(0, 2, 1, 3),
        "ctxT": by_channel(arr("ctx_2048").reshape(ROWS, CW).T, KC),
        "kvw": np.stack(kvw),
        "wqA": halves(two("Wq", A), XC),
        "woA": halves(two("Wo", A), 8),
        "wqB": np.stack([by_channel(w, XC).reshape(P, 2048) for w in two("wq", BB)]),
        "woB": np.stack([by_channel(w, XC).reshape(P, 2048) for w in two("wo", BB)]),
        "boA": two("bo", A).reshape(PAIRS, XC, P).transpose(2, 0, 1),
        "normB": two("norm_w", BB).reshape(PAIRS, XC, P).transpose(2, 0, 1),
        "masks": np.stack([arr("mask_S_fk1"), arr("mask_S_fk0")]),
        "tokens": np.ascontiguousarray(tokens).view(np.int32).reshape(1, -1),
    }
    nc = bacc.Bacc("TRN2", target_bir_lowering=False, num_devices=1)
    nc.disable_value_cache = True
    build(nc, words)
    r = run(nc, [{n: np.ascontiguousarray(a) for n, a in maps.items()}], core_ids=[0])
    out = r.results[0]["stream"]
    return np.ascontiguousarray(out.transpose(0, 2, 1, 3).reshape(B, D, TOK).transpose(0, 2, 1))
```

```python
from contextlib import ExitStack

import concourse.bass as bass
from concourse import mybir

F32 = mybir.dt.float32
F32R = mybir.dt.float32r
I32 = mybir.dt.int32
ALU = mybir.AluOpType
ACT = mybir.ActivationFunctionType
AX_X = mybir.AxisListType.X

P = 128
B, TOK, D = 8, 512, 512
CTX, CW = 77, 1024
ROWS = B * CTX
KC = CW // P
XC = D // P
PAIRS = 2
GROUPS, GH = 4, 4
TILES = TOK // P
SC = GH * CTX
CH = -(-SC // 3)
CHUNK_ROWS = [min(CH, SC - CH * n) for n in range(3)]
PART = 2048
BLK = 256
HALF = ROWS // 2
SUPPRESS, EPS = 20.0, 1e-5
UNITS2 = 2 * GROUPS
VROWS = [min(P, ROWS - P * r) for r in range(-(-ROWS // P))]


class Kind:

    def __init__(self, name, heads_wide, kv_blocks, pieces, out_chunks):
        self.name = name
        self.Q = heads_wide
        self.blocks = kv_blocks
        self.pieces = pieces
        self.O = out_chunks
        self.DH = 128 * heads_wide // GH
        self.key_dmas = 2 if name == "A" else GH
        queries, acc = [], []
        for u in range(B * GROUPS):
            queries += [("q", u, m) for m in range(self.Q)]
            if name == "B" and u % GROUPS == 0:
                queries.append(("stats", u // GROUPS))
            acc += [("pv", u, m) for m in range(self.Q)]
            if u % GROUPS == GROUPS - 1:
                acc += [("proj", u // GROUPS, m) for m in range(XC)]
        self.at = {item: n for order in (queries, acc) for n, item in enumerate(order)}
        self.queries2, self.acc2 = len(queries) // (B // 2), len(acc) // (B // 2)


def value_pieces(width, outs):
    blocks, pieces = [], []
    for n in range(3):
        for h in range(GH):
            lo, hi = max(h * CTX, n * CH), min((h + 1) * CTX, n * CH + CHUNK_ROWS[n])
            if lo < hi:
                key = (n, h * outs // GH)
                if key not in blocks:
                    blocks.append(key)
                pieces.append((h, lo - h * CTX, hi - h * CTX, blocks.index(key), lo - n * CH))
    return blocks, pieces


KIND_A = Kind("A", 2, *value_pieces(64, 2), 8)
KIND_B = Kind("B", 1, *value_pieces(32, 1), 4)


def three_passes(pe, out, weights, moving, start, stop):
    pe.matmul(out, weights[0], moving[0], start=start, stop=False)
    pe.matmul(out, weights[0], moving[1], start=False, stop=False)
    return pe.matmul(out, weights[1], moving[0], start=False, stop=stop)


def wait_apart(eng, semaphore, value, seen):
    eng.wait_ge(semaphore, value)
    eng.sem_inc(seen, 1)


def context_block(nc, ctxT, kvw, k_scr, v_scr, k1_scr, v1_scr, x_in, stream):
    NJ = PAIRS * GROUPS
    with ExitStack() as ctx:
        def sb(name, shape, dt):
            return ctx.enter_context(nc.sbuf_tensor(name, shape, dt))

        def sem(name):
            return ctx.enter_context(nc.semaphore(name))

        ctx_raw = sb("ctx_raw", [P, KC, ROWS], F32)
        ctx_s = sb("ctx_s", [P, 2, KC, ROWS], F32R)
        w_raw = sb("kvw_raw", [P, 2, KC, BLK], F32)
        w_s = sb("kvw_s", [P, 2, 2, KC, BLK], F32R)
        k_out = sb("k_out", [P, 2, 2, ROWS], F32R)
        v_out = sb("v_out", [P, len(VROWS), 2, BLK], F32R)
        banks = [ctx.enter_context(nc.psum_tensor(f"ctx_bank{i}", [P, 512], F32)) for i in range(8)]

        ctx_loaded, w_loaded = sem("ctx_loaded"), [sem("kw_loaded"), sem("vw_loaded")]
        ctx_hi, ctx_lo = sem("ctx_hi"), sem("ctx_lo")
        w_hi, w_lo = [sem("kw_hi"), sem("vw_hi")], [sem("kw_lo"), sem("vw_lo")]
        k_mm, v_mm = sem("k_mm"), sem("v_mm")
        k_hi, k_lo, v_hi, v_lo = sem("k_hi"), sem("k_lo"), sem("v_hi"), sem("v_lo")
        k_stored, v_stored, x_copied = sem("k_stored"), sem("v_stored"), sem("x_copied")
        sp_seen = sem("ctx_sp_seen")
        NV = len(VROWS)
        FULL = sum(r == P for r in VROWS)

        block = ctx.enter_context(nc.Block())

        @block.sync
        def _(sp):
            for counted in (k_lo, v_lo, k_stored, v_stored):
                sp.sem_inc(counted, 1)
            sp.dma_start(ctx_raw[:, :, :], ctxT).then_inc(ctx_loaded, 16)
            for slot in range(2):
                sp.dma_start(w_raw[:, slot], kvw[slot]).then_inc(w_loaded[slot], 16)
            sp.dma_start(stream, x_in).then_inc(x_copied, 16)
            with sp.Fori(0, NJ) as j:
                for slot in range(2):
                    wait_apart(sp, w_hi[slot], j + 1, sp_seen)
                    wait_apart(sp, w_lo[slot], j + 1, sp_seen)
                    sp.dma_start(w_raw[:, slot], kvw[2 * j + 2 + slot]).then_inc(w_loaded[slot], 16)
                for m in range(2):
                    wait_apart(sp, k_lo, 4 * j + 2 * m + 3, sp_seen)
                    for h in range(2):
                        sp.dma_start(k_scr[j, :, :, m, h].rearrange("b q n -> q b n"),
                                     k_out[:, m, h].bitcast(F32).rearrange("q (b n) -> q b n", b=B))\
                          .then_inc(k_stored, 16)
                wait_apart(sp, v_lo, NV * j + NV + 1, sp_seen)
                sp.dma_start(v_scr[j, 0:FULL * P].rearrange("(r p) s n -> p r s n", p=P),
                             v_out[:, 0:FULL].bitcast(F32)).then_inc(v_stored, 16)
                sp.dma_start(v_scr[j, FULL * P:ROWS], v_out[0:VROWS[-1], FULL].bitcast(F32)).then_inc(v_stored, 16)
            for p in range(PAIRS):
                sp.wait_ge(k_lo, 4 * NJ + 2 * p + 3)
                for h in range(2):
                    sp.dma_start(k1_scr[p, :, :, h].rearrange("b q n -> q b n"),
                                 k_out[:, p, h].bitcast(F32).rearrange("q (b n) -> q b n", b=B))\
                      .then_inc(k_stored, 16)
                sp.wait_ge(v_lo, NV * (NJ + p + 1) + 1)
                for h in range(2):
                    sp.dma_start(v1_scr[p, 0:FULL * P, h].rearrange("(r p) n -> p r n", p=P),
                                 v_out[:, 0:FULL, h, 0:P].bitcast(F32)).then_inc(v_stored, 16)
                sp.dma_start(v1_scr[p, FULL * P:ROWS],
                             v_out[0:VROWS[-1], FULL, :, 0:P].bitcast(F32)).then_inc(v_stored, 16)
            sp.wait_ge(k_stored, 64 * NJ + 32 * PAIRS + 1)
            sp.wait_ge(v_stored, 32 * NJ + 48 * PAIRS + 1)
            sp.wait_ge(x_copied, 16)

        @block.scalar
        def _(act):
            def split_weights(slot, j):
                act.wait_ge(w_loaded[slot], 16 * j + 16)
                if slot == 0:
                    act.wait_ge(k_mm, 4 * j)
                else:
                    act.wait_ge(v_mm, NV * j)
                act.activation(w_s[:, slot, 0], w_raw[:, slot], ACT.Copy).then_inc(w_hi[slot], 1)

            def drain_keys(n, j, stored):
                m, h = n // 2, n % 2
                act.wait_ge(k_mm, 4 * j + n + 1)
                if n == 0:
                    act.wait_ge(k_stored, stored + 1)
                act.activation(k_out[:, m, 0, h * HALF:(h + 1) * HALF], banks[n][:, 0:HALF], ACT.Copy)\
                   .then_inc(k_hi, 1)

            def drain_values(r, item, width, stored):
                act.wait_ge(v_mm, item + 1)
                if r == 0:
                    act.wait_ge(v_stored, stored + 1)
                act.activation(v_out[0:VROWS[r], r, 0, 0:width], banks[4 + r % 4][0:VROWS[r], 0:width], ACT.Copy)\
                   .then_inc(v_hi, 1)

            act.wait_ge(ctx_loaded, 16)
            for k in range(KC):
                act.activation(ctx_s[:, 0, k], ctx_raw[:, k], ACT.Copy).then_inc(ctx_hi, 1)
            split_weights(0, 0)
            split_weights(1, 0)
            with act.Fori(0, NJ) as j:
                for n in range(4):
                    drain_keys(n, j, 64 * j)
                split_weights(0, j + 1)
                for r in range(NV):
                    drain_values(r, NV * j + r, BLK, 32 * j)
                split_weights(1, j + 1)
            for p in range(PAIRS):
                for h in range(2):
                    drain_keys(2 * p + h, NJ, 64 * NJ)
                for r in range(NV):
                    drain_values(r, NV * (NJ + p) + r, P, 32 * NJ + 48 * p)

        @block.vector
        def _(dve):
            def split_weights(slot, j):
                dve.wait_ge(w_hi[slot], j + 1)
                dve.tensor_tensor(w_s[:, slot, 1], w_raw[:, slot], w_s[:, slot, 0].bitcast(F32), ALU.subtract)\
                   .then_inc(w_lo[slot], 1)

            def drain_keys(n, j):
                m, h = n // 2, n % 2
                dve.wait_ge(k_hi, 4 * j + n + 1)
                dve.tensor_tensor(k_out[:, m, 1, h * HALF:(h + 1) * HALF], banks[n][:, 0:HALF],
                                  k_out[:, m, 0, h * HALF:(h + 1) * HALF].bitcast(F32), ALU.subtract)\
                   .then_inc(k_lo, 1)

            def drain_values(r, item, width):
                dve.wait_ge(v_hi, item + 1)
                dve.tensor_tensor(v_out[0:VROWS[r], r, 1, 0:width], banks[4 + r % 4][0:VROWS[r], 0:width],
                                  v_out[0:VROWS[r], r, 0, 0:width].bitcast(F32), ALU.subtract).then_inc(v_lo, 1)

            for k in range(KC):
                dve.wait_ge(ctx_hi, k + 1)
                dve.tensor_tensor(ctx_s[:, 1, k], ctx_raw[:, k], ctx_s[:, 0, k].bitcast(F32), ALU.subtract)\
                   .then_inc(ctx_lo, 1)
            split_weights(0, 0)
            split_weights(1, 0)
            with dve.Fori(0, NJ) as j:
                for n in range(4):
                    drain_keys(n, j)
                split_weights(0, j + 1)
                for r in range(NV):
                    drain_values(r, NV * j + r, BLK)
                split_weights(1, j + 1)
            for p in range(PAIRS):
                for h in range(2):
                    drain_keys(2 * p + h, NJ)
                for r in range(NV):
                    drain_values(r, NV * (NJ + p) + r, P)

        @block.tensor
        def _(pe):
            def keys(n, slot, col):
                h = n % 2
                for k in range(KC):
                    mm = three_passes(pe, banks[n][:, 0:HALF],
                                      [w_s[:, slot, s, k, col:col + P] for s in range(2)],
                                      [ctx_s[:, s, k, h * HALF:(h + 1) * HALF] for s in range(2)],
                                      k == 0, k == KC - 1)
                mm.then_inc(k_mm, 1)

            def values(r, slot, col, width):
                for k in range(KC):
                    mm = three_passes(pe, banks[4 + r % 4][0:VROWS[r], 0:width],
                                      [ctx_s[:, s, k, r * P:r * P + VROWS[r]] for s in range(2)],
                                      [w_s[:, slot, s, k, col:col + width] for s in range(2)],
                                      k == 0, k == KC - 1)
                mm.then_inc(v_mm, 1)

            pe.wait_ge(ctx_lo, KC)
            with pe.Fori(0, NJ) as j:
                pe.wait_ge(w_lo[0], j + 1)
                for n in range(4):
                    pe.wait_ge(k_lo, 4 * j + 1)
                    keys(n, 0, (n // 2) * P)
                pe.wait_ge(w_lo[1], j + 1)
                for r in range(NV):
                    pe.wait_ge(v_lo, NV * j + (2 if r == 4 else 1))
                    values(r, 1, 0, BLK)
            for p in range(PAIRS):
                pe.wait_ge(w_lo[p], NJ + 1)
                for h in range(2):
                    pe.wait_ge(k_lo, 4 * NJ + 1)
                    keys(2 * p + h, p, 0)
                for r in range(NV):
                    pe.wait_ge(v_lo, NV * (NJ + p) + (2 if r == 4 else 1))
                    values(r, p, P, P)


def attention_block(nc, stream, k_scr, v_scr, k1_scr, v1_scr, wqA, woA, wqB, woB, boA, normB, masks, tokens,
                    token_words):
    with ExitStack() as ctx:
        def sb(name, shape, dt):
            return ctx.enter_context(nc.sbuf_tensor(name, shape, dt))

        def sem(name):
            return ctx.enter_context(nc.semaphore(name))

        x = sb("x", [P, 2, XC, TOK], F32)
        x_s = sb("x_s", [P, 2, XC, TOK], F32R)
        q_s = sb("q_s", [P, 2, 2, 2, TOK], F32R)
        prob = sb("prob", [P, 2, TILES, SC], F32)
        pT_s = sb("pT_s", [P, 3, 2, TOK], F32R)
        o_s = sb("o_s", [P, 2, 8, TOK], F32R)
        w_s = sb("w_s", [P, 4, 2, PART], F32R)
        stage = sb("stage", [P, PART], F32)
        xsq = sb("xsq", [P, XC, TOK], F32)
        keys_s = sb("keys_s", [P, 2, 2 * SC], F32R)
        vals_s = sb("vals_s", [P, 2, 4, 2, P], F32R)
        x_power = sb("x_power", [P, TOK], F32)
        ident = sb("ident", [P, P], F32)
        mean_w = sb("mean_w", [P, 1], F32)
        mhalf = sb("mhalf", [P, TILES], F32)
        mask_s = sb("mask_s", [P, TOK], F32R)
        hit_s = sb("hit_s", [P, PAIRS, SC], F32R)
        bo = sb("bo", [P, PAIRS, XC], F32)
        nw = sb("nw", [P, PAIRS, XC], F32)
        mx = sb("mx", [P, 2, 4 * GH], F32)
        sums = sb("sums", [P, 2, 4 * GH], F32)
        rinv = sb("rinv", [P, 2, 4 * GH], F32)
        ms = sb("ms", [P, 2, TILES], F32)
        rstd = sb("rstd", [P, 2, TILES], F32)
        hit_now = sb("hit_now", [P, SC], F32R)
        bo_now = sb("bo_now", [P, XC], F32)
        nw_now = sb("nw_now", [P, XC], F32)
        tok_i = sb("tok_i", [P, 8], I32)
        tok_f = sb("tok_f", [P, 2, 8], F32)
        mask_raw, mask_b = xsq[:, 0], xsq[:, 1]
        iota_t = xsq[:, 2, 0:CTX]
        cmp_t = [xsq[:, 2, CTX * (1 + n):CTX * (2 + n)] for n in range(4)]

        def bank(name):
            return ctx.enter_context(nc.psum_tensor(name, [P, 512], F32))

        q_bank = [bank("q_bank0"), bank("q_bank1")]
        s_bank = [bank("s_bank0"), bank("s_bank1")]
        t_bank = [bank("t_bank0"), bank("t_bank1")]
        acc_bank = [bank("acc_bank0"), bank("acc_bank1")]

        consts, cleared, setup_loaded = sem("consts"), sem("setup_cleared"), sem("setup_loaded")
        chain, setup_done, zeroed, picked = sem("dve_chain"), sem("setup_done"), sem("kv_zeroed"), sem("layer_picked")

        sp_seen, pool_seen = sem("sp_seen"), sem("pool_seen")

        class Sems:
            def __init__(self, k):
                self.all = []

                def named(name):
                    self.all.append(sem(f"{k}_{name}"))
                    return self.all[-1]
                self.x_loaded = [named(f"x_loaded{k}") for k in range(XC)]
                self.x_hi, self.x_sq, self.x_power = map(named, ("x_hi", "x_sq", "x_power"))
                self.x_lo = [named("x_lo_dve"), named("x_lo_pool")]
                self.keys_loaded = [named("keys_loaded0"), named("keys_loaded1")]
                self.vals_loaded = [named("vals_loaded0"), named("vals_loaded1")]
                self.q_mm, self.q_hi, self.q_out = map(named, ("q_mm", "q_hi", "q_out"))
                self.s_mm, self.s_max, self.s_sub = map(named, ("s_mm", "s_max", "s_sub"))
                self.p_exp, self.p_sum, self.p_inv, self.p_norm = map(named, ("p_exp", "p_sum", "p_inv", "p_norm"))
                self.t_mm, self.t_hi, self.t_lo = map(named, ("t_mm", "t_hi", "t_lo"))
                self.acc_mm, self.o_hi, self.acc_out = map(named, ("acc_mm", "o_hi", "acc_out"))
                self.rstd_ready = named("rstd_ready")
                self.stored = [named(f"stored{k}") for k in range(XC)]

        sems = {"A": Sems("A"), "B": Sems("B")}
        w_loaded, w_scaled, w_hi, w_lo = map(sem, ("w_loaded", "w_scaled", "w_hi", "w_lo"))
        AHEAD, PER_PAIR = 2, 6

        def weight_count(p, n):
            return PER_PAIR * p + (AHEAD + n + 2)

        def upto(J, per_unit, s, n):
            return J * (UNITS2 * per_unit) + (per_unit * s + n + 1)

        def acc_upto(kind, J, item):
            return J * kind.acc2 + (kind.at[item] + 2)

        def query_upto(kind, J, item):
            return J * kind.queries2 + (kind.at[item] + 2)

        SPLIT_ORDER = (0, 2, 1, 3)

        def x_lo_part(eng, S, J, b, k):
            eng.wait_ge(S.x_hi, 8 * J + (4 * b + SPLIT_ORDER.index(k) + 2))
            eng.tensor_tensor(x_s[:, 1, k], x[:, b % 2, k], x_s[:, 0, k].bitcast(F32), ALU.subtract)\
               .then_inc(S.x_lo[k // 2], 1)

        def layer_before(kind, p):
            return (sems["A"], KIND_A, 4 * p + 4) if kind.name == "B" else (sems["B"], KIND_B, 4 * p)

        def layer_after(kind, p):
            return (sems["B"], 4 * p) if kind.name == "A" else (sems["A"], 4 * p + 4)

        def pipeline(eng, p, first, step, weights=None):
            first()
            for s in range(2):
                step(4 * p, s, False)
                if weights:
                    weights(False, s)
            with eng.Fori(0, B // 2 - 1) as it:
                J = 4 * p + it
                for s in range(2, UNITS2 + 2):
                    step(J, s, False)
            for s in range(2, UNITS2 + 2):
                step(4 * p + (B // 2 - 1), s, True)
                if weights:
                    weights(True, s)

        SPLITS = {"A": {(False, 0): (0, 2), (False, 1): (1, 3), (True, 7): (2, 0)},
                  "B": {(False, 1): (3, 2), (True, 5): (4, 1), (True, 7): (5, 0)}}

        def parts(s, ends):
            return exists(s, ends), exists(s + 1, ends), s >= 1 and exists(s - 1, ends), s > GROUPS and s % GROUPS == 1

        def exists(s, ends):
            return s < UNITS2 or not ends

        block = ctx.enter_context(nc.Block())

        @block.sync
        def _(sp):
            for S in sems.values():
                for counted in S.all:
                    sp.sem_inc(counted, 1)
            for counted in (w_loaded, w_scaled, w_hi, w_lo):
                sp.sem_inc(counted, 1)
            sp.wait_ge(cleared, 1)
            sp.dma_start(mask_raw[0:1], masks[0:1]).then_inc(setup_loaded, 16)
            sp.dma_start(mask_raw[32:33], masks[0:1]).then_inc(setup_loaded, 16)
            sp.dma_start(mask_raw[64:65], masks[1:2]).then_inc(setup_loaded, 16)
            sp.dma_start(mask_raw[96:97], masks[1:2]).then_inc(setup_loaded, 16)
            sp.dma_start(tok_i[:, :], tokens[:, ::token_words].partition_broadcast(P)).then_inc(setup_loaded, 16)
            sp.dma_start(bo[:, :, :], boA).then_inc(setup_loaded, 16)
            sp.dma_start(nw[:, :, :], normB).then_inc(setup_loaded, 16)

            def load_weights(src):
                sp.dma_start(stage[:, :], src).then_inc(w_loaded, 16)

            def load_x(S, b, slot, k):
                sp.dma_start(x[:, slot, k], stream[b][:, k]).then_inc(S.x_loaded[k], 16)

            def load_keys(kind, p, s, b):
                g, slot, loaded = s % GROUPS, s % 2, sems[kind.name].keys_loaded[s % 2]
                if kind.name == "A":
                    keys = keys_s[:, slot].bitcast(F32).rearrange("q (c n) -> q c n", c=4)
                    for e in range(2):
                        sp.dma_start(keys[64 * e:64 * e + 64, :, CTX * e:CTX * e + CTX],
                                     k_scr[4 * p + g, b, 64 * e:64 * e + 64].rearrange("q c h n -> q (c h) n"))\
                          .then_inc(loaded, 16)
                else:
                    keys = keys_s[:, slot].bitcast(F32).rearrange("q (h n) -> q h n", h=2)
                    for r in range(GH):
                        sp.dma_start(keys[32 * r:32 * r + 32, :, CTX * r:CTX * r + CTX],
                                     k1_scr[p, b, 32 * g:32 * g + 32]).then_inc(loaded, 16)

            def load_vals(kind, p, s, b):
                g, slot, w = s % GROUPS, s % 2, kind.DH
                vals = vals_s[:, slot].bitcast(F32)
                for h, t0, t1, blk, row in kind.pieces:
                    src = (v_scr[4 * p + g, b, t0:t1, :, w * h:w * h + w] if kind.name == "A"
                           else v1_scr[p, b, t0:t1, :, w * g:w * g + w])
                    col = w * h % P
                    sp.dma_start(vals[row:row + t1 - t0, blk, :, col:col + w], src)\
                      .then_inc(sems[kind.name].vals_loaded[slot], 16)

            def first_units(kind, p, zeroed_before):
                wait_apart(sp, zeroed, zeroed_before + 2, sp_seen)
                for s in range(2):
                    load_keys(kind, p, s, 0)
                    load_vals(kind, p, s, 0)

            def layer(kind, p):
                S = sems[kind.name]

                def step(J, s, it, ends):
                    finished = parts(s, ends)[3]
                    b = s // GROUPS - 1

                    def store(m):
                        wait_apart(sp, S.acc_out, acc_upto(kind, J, ("proj", b, m)), sp_seen)
                        sp.dma_start(stream[2 * it + b][:, m], x[:, b % 2, m]).then_inc(S.stored[m], 16)

                    if ends and s == UNITS2 + 1:
                        first_units(*((KIND_B, p, 4 * p + 2) if kind.name == "A" else (KIND_A, 1 - p, 4 * p + 4)))
                    if finished:
                        store(0)
                    if exists(s + 2, ends):
                        wait_apart(sp, S.s_mm, upto(J, TILES, s, TILES), sp_seen)
                        load_keys(kind, p, s + 2, 2 * it + (s + 2) // GROUPS)
                    if finished:
                        for m in range(1, XC):
                            store(m)
                        for k in range(XC):
                            wait_apart(sp, S.stored[k], 32 * J + (16 * (b + 1) + 1), sp_seen)
                            if ends:
                                after, J2 = layer_after(kind, p)
                                if b == 1:
                                    wait_apart(sp, after.x_loaded[k], 32 * J2 + 17, sp_seen)
                                load_x(after, b, b, k)
                            else:
                                wait_apart(sp, S.x_loaded[k], 32 * J + (16 * (b + 2) + 1), sp_seen)
                                load_x(S, 2 * it + b + 2, b % 2, k)
                    if s >= 1 and exists(s + 1, ends):
                        wait_apart(sp, S.acc_mm, acc_upto(kind, J, ("pv", s - 1, kind.Q - 1)), sp_seen)
                        load_vals(kind, p, s + 1, 2 * it + (s + 1) // GROUPS)

                def weights(tail, s):
                    if (tail, s) in SPLITS[kind.name]:
                        n = SPLITS[kind.name][(tail, s)][0]
                        wait_apart(sp, w_lo, weight_count(p, n), sp_seen)
                        load_weights((woA[p, 1], wqB[p], woB[p], wqA[1 - p, 1], wqA[1 - p, 0], woA[1 - p, 0])[n])

                for s in range(2):
                    step(4 * p, s, 0, False)
                    weights(False, s)
                with sp.Fori(0, B // 2 - 1) as it:
                    J = 4 * p + it
                    for s in range(2, UNITS2 + 2):
                        step(J, s, it, False)
                last = B // 2 - 1
                for s in range(2, UNITS2 + 2):
                    step(4 * p + last, s, last, True)
                    weights(True, s)

            for b in range(2):
                for k in range(XC):
                    if b == 1:
                        sp.wait_ge(sems["A"].x_loaded[k], 17)
                    load_x(sems["A"], b, b, k)
            sp.wait_ge(zeroed, 2)
            for s in range(2):
                load_keys(KIND_A, 0, s, 0)
                load_vals(KIND_A, 0, s, 0)
            for n, src in enumerate((wqA[0, 1], wqA[0, 0], woA[0, 0])):
                if n:
                    sp.wait_ge(w_lo, n + 1)
                load_weights(src)
            with sp.Fori(0, PAIRS) as p:
                layer(KIND_A, p)
                layer(KIND_B, p)

            sp.wait_ge(w_loaded, 16 * (AHEAD + 1 + PER_PAIR * PAIRS) + 1)
            for k in range(XC):
                sp.wait_ge(sems["A"].x_loaded[k], 16 * B * PAIRS + 33)
            for slot in range(2):
                sp.wait_ge(sems["A"].keys_loaded[slot], 16 * KIND_A.key_dmas * (B * GROUPS // 2 * PAIRS + 1) + 1)
                sp.wait_ge(sems["A"].vals_loaded[slot], 16 * len(KIND_A.pieces) * (B * GROUPS // 2 * PAIRS + 1) + 1)

        @block.tensor
        def _(pe):
            def layer(kind, p):
                S = sems[kind.name]
                Q, a = kind.Q, kind.name == "A"
                if a:
                    wq = [[w_s[:, k // 2, h, 1024 * (k % 2):1024 * (k % 2) + 1024] for h in range(2)] for k in range(XC)]
                    wo = [[w_s[:, 2 + k // 4, h, 512 * (k % 4):512 * (k % 4) + 512] for h in range(2)] for k in range(8)]
                else:
                    wq = [[w_s[:, 0, h, 512 * k:512 * k + 512] for h in range(2)] for k in range(XC)]
                    wo = [[w_s[:, 2, h, 512 * k:512 * k + 512] for h in range(2)] for k in range(XC)]

                def scores(J, s, t):
                    slot = s % 2
                    if t == 0:
                        pe.wait_ge(S.q_out, query_upto(kind, J, ("q", s, Q - 1)))
                        pe.wait_ge(S.keys_loaded[slot], (J * 4 + (s // 2 + 1)) * (16 * kind.key_dmas) + 1)
                    if 4 * s + t >= 2:
                        pe.wait_ge(S.s_sub, upto(J, TILES, s, t - 1))
                    out = s_bank[t % 2]
                    tok = slice(t * P, t * P + P)
                    if a:
                        pe.matmul(out[:, 0:SC], mask_s[:, tok], hit_now[:, :], start=True, stop=False)
                        keys = keys_s[:, slot].rearrange("q (c h n) -> q c h n", c=2, h=2)
                        for c in range(2):
                            mm = three_passes(pe, out[:, 2 * CTX * c:2 * CTX * (c + 1)],
                                              [q_s[:, slot, h, c, tok] for h in range(2)],
                                              [keys[:, c, h] for h in range(2)], False, c == 1)
                    else:
                        keys = keys_s[:, slot].rearrange("q (h n) -> q h n", h=2)
                        mm = three_passes(pe, out[:, 0:SC], [q_s[:, slot, h, 0, tok] for h in range(2)],
                                          [keys[:, h] for h in range(2)], True, True)
                    mm.then_inc(S.s_mm, 1)

                def queries(J, s, m, chunks):
                    item = kind.at[("q", s, m)]
                    if 0 in chunks and item >= 2:
                        pe.wait_ge(S.q_out, J * kind.queries2 + item)
                    col = (s % GROUPS * Q + m) * P
                    for k in chunks:
                        if s % GROUPS == 0 and m == 0:
                            pe.wait_ge(S.x_lo[k // 2], 4 * J + (2 * (s // GROUPS) + k % 2 + 2))
                        mm = three_passes(pe, q_bank[item % 2][:, :], [w[:, col:col + P] for w in wq[k]],
                                          [x_s[:, h, k] for h in range(2)], k == 0, k == XC - 1)
                    if XC - 1 in chunks:
                        mm.then_inc(S.q_mm, 1)

                def turn(J, s, n):
                    if n == 0:
                        pe.wait_ge(S.p_norm, upto(J, 1, s, 1))
                    pe.wait_ge(S.t_lo, upto(J, 3, s, n - 1 if 3 * s + n >= 1 else 0))
                    rows = CHUNK_ROWS[n]
                    for t in range(TILES):
                        mm = pe.transpose(t_bank[(3 * s + n) % 2][0:rows, t * P:t * P + P],
                                          prob[:, s % 2, t, CH * n:CH * n + rows], ident[:, :])
                    mm.then_inc(S.t_mm, 1)

                def acc_free(J, item):
                    n = kind.at[item]
                    pe.wait_ge(S.acc_out, J * kind.acc2 + max(n, 1))
                    return acc_bank[n % 2]

                def values(J, s, m):
                    out = acc_free(J, ("pv", s, m))
                    if m == 0:
                        pe.wait_ge(S.vals_loaded[s % 2], (J * 4 + (s // 2 + 1)) * (16 * len(kind.pieces)) + 1)
                    mine = [i for i, (_, o) in enumerate(kind.blocks) if o == m]
                    for i in mine:
                        n = kind.blocks[i][0]
                        rows = CHUNK_ROWS[n]
                        pe.wait_ge(S.t_lo, upto(J, 3, s, n + 1))
                        mm = three_passes(pe, out[:, :], [vals_s[0:rows, s % 2, i, h] for h in range(2)],
                                          [pT_s[0:rows, n, h] for h in range(2)], i == mine[0], i == mine[-1])
                    mm.then_inc(S.acc_mm, 1)

                def project(J, b, m):
                    out = acc_free(J, ("proj", b, m))
                    if m == 0:
                        pe.wait_ge(w_lo, weight_count(p, 1 if a else 3))
                    for k in range(kind.O):
                        if m == 0 and k >= kind.O - Q:
                            pe.wait_ge(S.acc_out, acc_upto(kind, J, ("pv", GROUPS * b + GROUPS - 1, k - (kind.O - Q))))
                        mm = three_passes(pe, out[:, :], [w[:, m * P:m * P + P] for w in wo[k]],
                                          [o_s[:, h, k] for h in range(2)], k == 0, k == kind.O - 1)
                    mm.then_inc(S.acc_mm, 1)

                def stats(J, b):
                    item = kind.at[("stats", b)]
                    out = q_bank[item % 2]
                    pe.wait_ge(S.q_out, J * kind.queries2 + item)
                    pe.wait_ge(S.x_power, 6 * J + (3 * b + 3 + 1))
                    for t in range(TILES):
                        mm = pe.matmul(out[:, t:t + 1], x_power[:, t * P:t * P + P], mean_w[:, :],
                                       start=t == 0, stop=t == TILES - 1, skip_group_check=True)
                    mm.then_inc(S.q_mm, 1)

                def first():
                    before, K, J2 = layer_before(kind, p)
                    pe.wait_ge(w_lo, weight_count(p, -1 if a else 2))
                    pe.wait_ge(before.q_out, K.queries2 * J2 + 1)
                    pe.wait_ge(before.s_sub, UNITS2 * TILES * J2 + 1)
                    pe.wait_ge(before.t_lo, UNITS2 * 3 * J2 + 1)
                    for m in range(Q):
                        queries(4 * p, 0, m, range(XC))
                    pe.wait_ge(before.acc_out, K.acc2 * J2 + 1)
                    if a:
                        pe.wait_ge(picked, 3 * p + 3)
                    if not a:
                        stats(4 * p, 0)

                def step(J, s, ends):
                    live, has_next, has_last, finished = parts(s, ends)
                    early = not a and s % GROUPS == 2

                    def next_queries(m, chunks):
                        if has_next:
                            queries(J, s + 1, m, chunks)

                    def projection(m):
                        if finished:
                            project(J, s // GROUPS - 1, m)

                    if live:
                        scores(J, s, 0)
                        scores(J, s, 1)
                    projection(0)
                    next_queries(0, range(XC) if a or early else range(2))
                    if early and has_last:
                        turn(J, s - 1, 0)
                        turn(J, s - 1, 1)
                    if live:
                        scores(J, s, 2)
                        scores(J, s, 3)
                    projection(1)
                    if not early and has_last:
                        turn(J, s - 1, 0)
                        turn(J, s - 1, 1)
                    projection(2)
                    if not early:
                        next_queries(Q - 1, range(XC) if a else range(2, XC))
                    if has_last:
                        turn(J, s - 1, 2)
                    projection(3)
                    if has_last:
                        for m in range(Q):
                            values(J, s - 1, m)
                    if not a and s % GROUPS == GROUPS - 1 and has_next:
                        stats(J, (s + 1) // GROUPS)

                pipeline(pe, p, first, step)

            pe.wait_ge(consts, 4)
            pe.wait_ge(setup_done, 1)
            with pe.Fori(0, PAIRS) as p:
                layer(KIND_A, p)
                layer(KIND_B, p)

        @block.scalar
        def _(act):
            def layer(kind, p):
                S = sems[kind.name]
                Q, a = kind.Q, kind.name == "A"

                def split_x(S, J, b, chunks):
                    for k in chunks:
                        act.wait_ge(S.x_loaded[k], 32 * J + (16 * (b + 1) + 1))
                        act.activation(x_s[:, 0, k], x[:, b % 2, k], ACT.Copy).then_inc(S.x_hi, 1)

                def square_x(S, J, b, chunks):
                    for k in chunks:
                        if b >= 1 and k == 0:
                            act.wait_ge(S.x_power, 6 * J + (3 * b + 1))
                        act.activation(xsq[:, k], x[:, b % 2, k], ACT.Square).then_inc(S.x_sq, 1)

                def exps(J, s, half):
                    tiles = range(2 * half, 2 * half + 2)
                    if a:
                        act.wait_ge(S.s_sub, upto(J, TILES, s, 2 * half + 2))
                        act.activation(prob[:, s % 2, 2 * half:2 * half + 2], prob[:, s % 2, 2 * half:2 * half + 2],
                                       ACT.Exp, scale=float(kind.DH) ** -0.5).then_inc(S.p_exp, 1)
                        return
                    if half == 0:
                        act.wait_ge(S.rstd_ready, 2 * J + (s // GROUPS + 2))
                    for t in tiles:
                        act.wait_ge(S.s_sub, upto(J, TILES, s, t + 1))
                        e = act.activation(prob[:, s % 2, t], prob[:, s % 2, t], ACT.Exp,
                                           scale=rstd[:, s // GROUPS % 2, t:t + 1])
                    e.then_inc(S.p_exp, 1)

                def q_hi(J, s, m):
                    act.wait_ge(S.q_mm, query_upto(kind, J, ("q", s, m)))
                    if m == 0 and s >= 1:
                        act.wait_ge(S.s_mm, upto(J, TILES, s - 1, 0))
                    act.activation(q_s[:, s % 2, 0, m], q_bank[kind.at[("q", s, m)] % 2][:, :], ACT.Copy)\
                       .then_inc(S.q_hi, 1)

                def t_hi(J, s, n):
                    act.wait_ge(S.t_mm, upto(J, 3, s, n + 1))
                    rows = CHUNK_ROWS[n]
                    act.activation(pT_s[0:rows, n, 0], t_bank[(3 * s + n) % 2][0:rows, :], ACT.Copy)\
                       .then_inc(S.t_hi, 1)

                def o_hi(J, s, m):
                    item = ("pv", s, m)
                    act.wait_ge(S.acc_mm, acc_upto(kind, J, item))
                    act.activation(o_s[:, 0, s % GROUPS * Q + m], acc_bank[kind.at[item] % 2][:, :], ACT.Copy)\
                       .then_inc(S.o_hi, 1)

                def first():
                    for m in range(Q):
                        q_hi(4 * p, 0, m)

                def step(J, s, ends):
                    live, has_next, has_last, _ = parts(s, ends)
                    new_x = s % GROUPS == 2
                    early = not a and new_x

                    def turned(n):
                        if has_last:
                            t_hi(J, s - 1, n)

                    def next_batch(n):
                        chunks = SPLIT_ORDER[2 * n:2 * n + 2]
                        if new_x and exists(s + 2, ends):
                            split_x(S, J, s // GROUPS + 1, chunks)
                        elif new_x:
                            split_x(*layer_after(kind, p), 0, chunks)

                    if live:
                        exps(J, s, 0)
                    if has_next and (a or early):
                        q_hi(J, s + 1, 0)
                    if not a and s % GROUPS == GROUPS - 1 and has_next:
                        square_x(S, J, s // GROUPS + 1, range(2, XC))
                    if a and live:
                        exps(J, s, 1)
                    turned(0)
                    turned(1)
                    if early:
                        next_batch(0)
                        turned(2)
                    if not a and live:
                        exps(J, s, 1)
                    if has_next and not early:
                        q_hi(J, s + 1, Q - 1)
                    if not early:
                        turned(2)
                        next_batch(0)
                    next_batch(1)
                    if has_last:
                        for m in range(Q):
                            o_hi(J, s - 1, m)
                    if not a and early and exists(s + 2, ends):
                        square_x(S, J, s // GROUPS + 1, range(2))
                    if a and ends and s == UNITS2 - 1:
                        square_x(*layer_after(kind, p), 0, range(XC))

                def weights(tail, s):
                    if (tail, s) in SPLITS[kind.name]:
                        n, part = SPLITS[kind.name][(tail, s)]
                        weights_hi(p, n, part, scaled=n == 2)

                pipeline(act, p, first, step, weights)

            def weights_hi(p, n, part, scaled=False):
                act.wait_ge(w_loaded, 16 * weight_count(p, n) - 15)
                if scaled:
                    act.wait_ge(w_scaled, p + 2)
                act.activation(w_s[:, part, 0], stage[:, :], ACT.Copy).then_inc(w_hi, 1)

            for k in SPLIT_ORDER:
                act.wait_ge(sems["A"].x_loaded[k], 17)
                act.activation(x_s[:, 0, k], x[:, 0, k], ACT.Copy).then_inc(sems["A"].x_hi, 1)
            for n, part in enumerate((1, 0)):
                weights_hi(0, n - AHEAD, part)
            with act.Fori(0, PAIRS) as p:
                layer(KIND_A, p)
                layer(KIND_B, p)

        @block.vector
        def _(dve):
            links = [0]

            def link(ins):
                links[0] += 1
                ins.then_inc(chain, 1)
                dve.wait_ge(chain, links[0])

            link(dve.memset(hit_s[:, :, :].bitcast(F32), 0.0))
            dve.wait_ge(consts, 5)
            dve.wait_ge(setup_loaded, 16 * 7)
            link(dve.tensor_scalar(mask_b, mask_raw, 1.0, SUPPRESS * float(KIND_A.DH) ** 0.5, ALU.subtract, ALU.mult))
            link(dve.tensor_copy(mask_s[:, :], mask_b))
            for row in (32, 96):
                link(dve.tensor_tensor(mask_s[row:row + 1, :], mask_b[row:row + 1], mask_s[row:row + 1, :].bitcast(F32),
                                       ALU.subtract))
            link(dve.tensor_copy(tok_f[:, 0, :], tok_i[:, :]))
            link(dve.tensor_scalar(tok_f[:, 1, :], tok_f[:, 0, :], float(CTX), None, ALU.add))
            for p in range(PAIRS):
                for which in range(2):
                    hits = [(w, 4 * p + 2 * which + i) for w in range(2) for i in range(2)]
                    for n, (w, i) in enumerate(hits):
                        if n == 0:
                            link(dve.tensor_scalar(cmp_t[which], iota_t, tok_f[:, w, i:i + 1], None, ALU.is_equal))
                        else:
                            link(dve.scalar_tensor_tensor(out=cmp_t[which], in0=iota_t, scalar=tok_f[:, w, i:i + 1],
                                                          in1=cmp_t[which], op0=ALU.is_equal, op1=ALU.max))
                link(dve.tensor_tensor(cmp_t[2], cmp_t[0], cmp_t[1], ALU.mult))
                link(dve.tensor_tensor(cmp_t[0], cmp_t[0], cmp_t[2], ALU.subtract))
                for row in (0, 32, 64, 96):
                    link(dve.tensor_copy(hit_s[row:row + 1, p].rearrange("q (h n) -> q h n", h=GH),
                                         cmp_t[row // 64][row:row + 1].unsqueeze(1).broadcast_to([1, GH, CTX])))
            dve.memset(bo_now[:, :], 0.0).then_inc(setup_done, 1)
            dve.wait_ge(setup_done, 1)

            def layer(kind, p):
                S = sems[kind.name]
                Q, a = kind.Q, kind.name == "A"

                def halves(J, s, half):
                    slot = s % 2
                    for t in (2 * half, 2 * half + 1):
                        dve.wait_ge(S.s_mm, upto(J, TILES, s, t + 1))
                        dve.tensor_reduce(mx[:, slot, GH * t:GH * t + GH],
                                          s_bank[t % 2][:, 0:SC].rearrange("q (h n) -> q h n", h=GH),
                                          AX_X, ALU.max).then_inc(S.s_max, 1)
                    for t in (2 * half, 2 * half + 1):
                        if t == 0 and s >= 1:
                            dve.wait_ge(S.t_mm, upto(J, 3, s - 1, 0))
                        dve.wait_ge(S.s_max, upto(J, TILES, s, t + 1))
                        dve.tensor_tensor(prob[:, slot, t].rearrange("q (h n) -> q h n", h=GH),
                                          s_bank[t % 2][:, 0:SC].rearrange("q (h n) -> q h n", h=GH),
                                          mx[:, slot, GH * t:GH * t + GH].unsqueeze(2).broadcast_to([P, GH, CTX]),
                                          ALU.subtract).then_inc(S.s_sub, 1)

                def q_lo(J, s, m):
                    dve.wait_ge(S.q_hi, upto(J, Q, s, m + 1))
                    dve.tensor_tensor(q_s[:, s % 2, 1, m], q_bank[kind.at[("q", s, m)] % 2][:, :],
                                      q_s[:, s % 2, 0, m].bitcast(F32), ALU.subtract).then_inc(S.q_out, 1)

                def t_lo(J, s, n):
                    rows = CHUNK_ROWS[n]
                    dve.wait_ge(S.t_hi, upto(J, 3, s, n + 1))
                    dve.tensor_tensor(pT_s[0:rows, n, 1], t_bank[(3 * s + n) % 2][0:rows, :],
                                      pT_s[0:rows, n, 0].bitcast(F32), ALU.subtract).then_inc(S.t_lo, 1)

                def o_lo(J, s, m):
                    c = s % GROUPS * Q + m
                    dve.wait_ge(S.o_hi, upto(J, Q, s, m + 1))
                    dve.tensor_tensor(o_s[:, 1, c], acc_bank[kind.at[("pv", s, m)] % 2][:, :],
                                      o_s[:, 0, c].bitcast(F32), ALU.subtract).then_inc(S.acc_out, 1)

                def denominators(J, s):
                    slot = s % 2
                    dve.wait_ge(S.p_exp, upto(J, 2, s, 2))
                    dve.tensor_reduce(sums[:, slot], prob[:, slot].rearrange("q t (h n) -> q (t h) n", h=GH),
                                      AX_X, ALU.add).then_inc(S.p_sum, 1)
                    dve.wait_ge(S.p_sum, upto(J, 1, s, 1))
                    dve.reciprocal(rinv[:, slot], sums[:, slot]).then_inc(S.p_inv, 1)

                def mean_squares(J, b):
                    item = ("stats", b)
                    dve.wait_ge(S.q_mm, query_upto(kind, J, item))
                    dve.tensor_scalar(ms[:, b % 2], q_bank[kind.at[item] % 2][:, 0:TILES], EPS * kind.DH, None,
                                      ALU.add).then_inc(S.q_out, 1)

                def add_result(J, b, m):
                    item = ("proj", b, m)
                    dve.wait_ge(S.acc_mm, acc_upto(kind, J, item))
                    out = acc_bank[kind.at[item] % 2][:, :]
                    if a:
                        dve.scalar_tensor_tensor(out=x[:, b % 2, m], in0=out, scalar=bo_now[:, m:m + 1],
                                                 in1=x[:, b % 2, m], op0=ALU.add, op1=ALU.add).then_inc(S.acc_out, 1)
                    else:
                        dve.tensor_tensor(x[:, b % 2, m], out, x[:, b % 2, m], ALU.add).then_inc(S.acc_out, 1)

                def first():
                    if a:
                        dve.tensor_copy(hit_now[:, :], hit_s[:, p].bitcast(F32)).then_inc(picked, 1)
                        dve.tensor_copy(bo_now[:, :], bo[:, p]).then_inc(picked, 1)
                        dve.tensor_copy(nw_now[:, :], nw[:, p]).then_inc(picked, 1)
                        dve.wait_ge(picked, 3 * p + 3)
                    for m in range(Q):
                        q_lo(4 * p, 0, m)
                    if not a:
                        mean_squares(4 * p, 0)

                def step(J, s, ends):
                    live, has_next, has_last, finished = parts(s, ends)
                    new_x = s % GROUPS == 2
                    early = not a and new_x

                    def result(m):
                        if finished:
                            add_result(J, s // GROUPS - 1, m)

                    if live:
                        halves(J, s, 0)
                    if not a and s >= 2:
                        o_lo(J, s - 2, 0)
                    result(0)
                    if has_next and a:
                        q_lo(J, s + 1, 0)
                    if has_last and early:
                        t_lo(J, s - 1, 0)
                        t_lo(J, s - 1, 1)
                    if live:
                        halves(J, s, 1)
                    result(1)
                    if has_last and not early:
                        t_lo(J, s - 1, 0)
                        t_lo(J, s - 1, 1)
                    result(2)
                    if has_next and not early:
                        q_lo(J, s + 1, Q - 1)
                    if has_last:
                        t_lo(J, s - 1, 2)
                    if has_next and early:
                        q_lo(J, s + 1, 0)
                    if new_x:
                        for k in range(2):
                            if exists(s + 2, ends):
                                x_lo_part(dve, S, J, s // GROUPS + 1, k)
                            else:
                                x_lo_part(dve, *layer_after(kind, p), 0, k)
                    if live:
                        denominators(J, s)
                    if not a and s % GROUPS == GROUPS - 1 and has_next:
                        mean_squares(J, (s + 1) // GROUPS)
                    result(3)
                    if a and has_last:
                        for m in range(Q):
                            o_lo(J, s - 1, m)

                def weights(tail, s):
                    if (tail, s) in SPLITS[kind.name]:
                        n, part = SPLITS[kind.name][(tail, s)]
                        if n == 2:
                            dve.wait_ge(w_loaded, 16 * weight_count(p, n) - 15)
                            for k in range(XC):
                                sc = dve.tensor_scalar(stage[:, 512 * k:512 * k + 512], stage[:, 512 * k:512 * k + 512],
                                                       nw_now[:, k:k + 1], None, ALU.mult)
                            sc.then_inc(w_scaled, 1)
                        weights_lo(p, n, part)

                pipeline(dve, p, first, step, weights)

            def weights_lo(p, n, part):
                dve.wait_ge(w_hi, weight_count(p, n))
                dve.tensor_tensor(w_s[:, part, 1], stage[:, :], w_s[:, part, 0].bitcast(F32), ALU.subtract)\
                   .then_inc(w_lo, 1)

            for k in range(2):
                x_lo_part(dve, sems["A"], 0, 0, k)
            for n, part in enumerate((1, 0)):
                weights_lo(0, n - AHEAD, part)
            with dve.Fori(0, PAIRS) as p:
                layer(KIND_A, p)
                layer(KIND_B, p)

        @block.gpsimd
        def _(pool):
            pool.memset(xsq[:, :, :], 0.0).then_inc(cleared, 1)
            pool.memset(ident[:, :], 0.0).then_inc(consts, 1)
            pool.memset(mean_w[:, :], KIND_B.DH / D).then_inc(consts, 1)
            pool.memset(mhalf[:, :], -0.5).then_inc(consts, 1)
            pool.wait_ge(consts, 3)
            pool.wait_ge(cleared, 1)
            pool.affine_select(out=ident[:, :], in_=ident[:, :], compare_op=ALU.not_equal, fill=1.0, base=0,
                               pattern=[[-1, P]], channel_multiplier=1).then_inc(consts, 1)
            pool.iota(iota_t, [[1, CTX]], base=0, channel_multiplier=0,
                      allow_small_or_imprecise_dtypes=True).then_inc(consts, 1)

            def layer(kind, p):
                S = sems[kind.name]
                a = kind.name == "A"

                def x_lo(S, J, b):
                    for k in (2, 3):
                        x_lo_part(pool, S, J, b, k)

                def sum_squares(S, J, b):
                    if b >= 1:
                        pool.wait_ge(S.q_mm, query_upto(kind, J, ("stats", b - 1)))
                    for k in range(1, XC):
                        pool.wait_ge(S.x_sq, 8 * J + (4 * b + k + 2))
                        if k > 1:
                            pool.wait_ge(S.x_power, 6 * J + (3 * b + k))
                        pool.tensor_tensor(x_power[:, :], xsq[:, 0] if k == 1 else x_power[:, :], xsq[:, k], ALU.add)\
                            .then_inc(S.x_power, 1)

                def normalise(J, s):
                    slot = s % 2
                    pool.wait_ge(S.p_inv, upto(J, 1, s, 1))
                    view = prob[:, slot].rearrange("q t (h n) -> q (t h) n", h=GH)
                    pool.tensor_tensor(view, view, rinv[:, slot].unsqueeze(2).broadcast_to([P, TILES * GH, CTX]),
                                       ALU.mult).then_inc(S.p_norm, 1)

                def root(J, b):
                    pool.wait_ge(S.q_out, query_upto(kind, J, ("stats", b)))
                    pool.tensor_tensor(rstd[:, b % 2], ms[:, b % 2], mhalf[:, :], ALU.pow).then_inc(S.rstd_ready, 1)

                def first():
                    if not a:
                        root(4 * p, 0)

                def step(J, s, ends):
                    new_stats = not a and s % GROUPS == GROUPS - 1 and exists(s + 1, ends)
                    if s % GROUPS == 2:
                        if exists(s + 2, ends):
                            x_lo(S, J, s // GROUPS + 1)
                        else:
                            x_lo(*layer_after(kind, p), 0)
                    if new_stats:
                        sum_squares(S, J, s // GROUPS + 1)
                    if new_stats:
                        root(J, (s + 1) // GROUPS)
                    if exists(s, ends):
                        normalise(J, s)
                    if a and ends and s == UNITS2 - 1:
                        sum_squares(*layer_after(kind, p), 0)
                    if ends and s == UNITS2:
                        wait_apart(pool, S.s_mm, upto(J, TILES, s - 1, TILES), pool_seen)
                        pool.memset(keys_s[:, :, :].bitcast(F32), 0.0).then_inc(zeroed, 1)
                        wait_apart(pool, S.acc_mm, acc_upto(kind, J, ("pv", s - 1, kind.Q - 1)), pool_seen)
                        pool.memset(vals_s[:, :, :, :, :].bitcast(F32), 0.0).then_inc(zeroed, 1)

                pipeline(pool, p, first, step)

            pool.memset(keys_s[:, :, :].bitcast(F32), 0.0).then_inc(zeroed, 1)
            pool.memset(vals_s[:, :, :, :, :].bitcast(F32), 0.0).then_inc(zeroed, 1)
            for k in (2, 3):
                x_lo_part(pool, sems["A"], 0, 0, k)
            with pool.Fori(0, PAIRS) as p:
                layer(KIND_A, p)
                layer(KIND_B, p)


def build(nc, words):
    def dram(name, shape, dt=F32, kind="ExternalInput"):
        return nc.dram_tensor(name, shape, dt, kind=kind).ap()

    x_in = dram("x_in", (B, P, XC, TOK))
    ctxT = dram("ctxT", (P, KC, ROWS))
    kvw = dram("kvw", (2 * PAIRS * GROUPS + 2, P, KC, BLK))
    wqA, woA = dram("wqA", (PAIRS, 2, P, 2048)), dram("woA", (PAIRS, 2, P, 2048))
    wqB, woB = dram("wqB", (PAIRS, P, 2048)), dram("woB", (PAIRS, P, 2048))
    boA, normB = dram("boA", (P, PAIRS, XC)), dram("normB", (P, PAIRS, XC))
    masks, tokens = dram("masks", (2, TOK)), dram("tokens", (1, 8 * words), I32)
    stream = dram("stream", (B, P, XC, TOK), kind="ExternalOutput")
    k_scr = dram("k_scr", (PAIRS * GROUPS, B, P, 2, 2, CTX), kind="Internal")
    v_scr = dram("v_scr", (PAIRS * GROUPS, ROWS, 2, BLK), kind="Internal")
    k1_scr = dram("k1_scr", (PAIRS, B, P, 2, CTX), kind="Internal")
    v1_scr = dram("v1_scr", (PAIRS, ROWS, 2, P), kind="Internal")
    context_block(nc, ctxT, kvw, k_scr, v_scr, k1_scr, v1_scr, x_in, stream)
    attention_block(nc, stream,
                    k_scr,
                    v_scr.rearrange("j (b t) s n -> j b t s n", b=B),
                    k1_scr,
                    v1_scr.rearrange("j (b t) s n -> j b t s n", b=B),
                    wqA, woA, wqB, woB, boA, normB, masks, tokens, words)


def kernel(**inputs):
    import numpy as np
    import concourse.bacc as bacc
    from concourse.bass_utils import run_bass_kernel_spmd as run

    def arr(name):
        return np.asarray(inputs[name])

    def by_channel(w, chunks):
        return w.reshape(chunks, P, -1).transpose(1, 0, 2)

    def blocks(w):
        return by_channel(w, KC).reshape(P, KC, -1, BLK).transpose(2, 0, 1, 3)

    kvw = []
    for l in ("L0", "L2"):
        k, v = blocks(arr(l + "_xattn_Wk")), blocks(arr(l + "_xattn_Wv"))
        for g in range(GROUPS):
            kvw += [k[g], v[g]]
    for l in ("L1", "L3"):
        kvw.append(blocks(np.concatenate([arr(l + "_xattn_wk"), arr(l + "_xattn_wv")], axis=1))[0])
    two = lambda name, pair: np.stack([arr(f"{l}_xattn_{name}") for l in pair])
    A, BB = ("L0", "L2"), ("L1", "L3")
    halves = lambda w, c: np.stack([by_channel(m, c).reshape(P, 2, 2048).transpose(1, 0, 2) for m in w])
    tokens = np.concatenate([arr(f"{l}_xattn_token_indices_{w}") for l in A for w in "AB"])
    words = tokens.dtype.itemsize // 4
    maps = {
        "x_in": arr("x").transpose(0, 2, 1).reshape(B, XC, P, TOK).transpose(0, 2, 1, 3),
        "ctxT": by_channel(arr("ctx_2048").reshape(ROWS, CW).T, KC),
        "kvw": np.stack(kvw),
        "wqA": halves(two("Wq", A), XC),
        "woA": halves(two("Wo", A), 8),
        "wqB": np.stack([by_channel(w, XC).reshape(P, 2048) for w in two("wq", BB)]),
        "woB": np.stack([by_channel(w, XC).reshape(P, 2048) for w in two("wo", BB)]),
        "boA": two("bo", A).reshape(PAIRS, XC, P).transpose(2, 0, 1),
        "normB": two("norm_w", BB).reshape(PAIRS, XC, P).transpose(2, 0, 1),
        "masks": np.stack([arr("mask_S_fk1"), arr("mask_S_fk0")]),
        "tokens": np.ascontiguousarray(tokens).view(np.int32).reshape(1, -1),
    }
    nc = bacc.Bacc("TRN2", target_bir_lowering=False, num_devices=1)
    nc.disable_value_cache = True
    build(nc, words)
    r = run(nc, [{n: np.ascontiguousarray(a) for n, a in maps.items()}], core_ids=[0])
    out = r.results[0]["stream"]
    return np.ascontiguousarray(out.transpose(0, 2, 1, 3).reshape(B, D, TOK).transpose(0, 2, 1))
```
